# Optimizing a Trainium2 kernel written in Bass

```python
import numpy as np
import jax
import jax.numpy as jnp

def _softmax(x, axis=-1):
    return jax.nn.softmax(x, axis=axis)

def _gelu(x):
    return jax.nn.gelu(x, approximate=True)

def _silu(x):
    return jax.nn.silu(x)

def _sigmoid(x):
    return jax.nn.sigmoid(x)

def _layernorm(x, axis=-1, eps=1e-05):
    m = jnp.mean(x, axis=axis, keepdims=True)
    v = jnp.var(x, axis=axis, keepdims=True)
    return (x - m) / jnp.sqrt(v + eps)

def _scatter_add(tgt, idx, src, axis=0):
    return tgt.at[idx].add(src)

def _segment_sum(src, seg, n):
    return jax.ops.segment_sum(src, seg, n)
kernel_name = 'mk_dlrm_tower_d1_rec_r8_52ee7f'

def setup_inputs(seed: int=0):
    np.random.seed(seed)
    _w = jnp.asarray

    def _rec_inputs():
        import jax
        import jax.numpy as jnp
        _tk = jax.random.key(seed)
        dense_ctx = jax.random.normal(jax.random.fold_in(_tk, 190), (2048, 16), jnp.float32)
        ids = jnp.stack([jax.random.randint(jax.random.fold_in(_tk, 200 + f), (2048,), 0, v, jnp.int32) for f, v in enumerate([1000, 1000, 1250, 1250, 12500, 1000, 125000, 125000, 1000, 125000, 1000, 125000, 1250, 125000, 1250, 125000, 1000, 1000, 125000, 12500, 12500, 1250, 1000, 1250, 1250, 1250, 1250, 1250, 12500, 12500, 1250, 1000, 1250, 1000, 1000, 12500, 1000, 1000, 1000, 1250])], axis=1)
        tbl_0 = 0.05 * jax.random.normal(jax.random.fold_in(_tk, 500 + 0), (1000, 32), jnp.float32)
        tbl_1 = 0.05 * jax.random.normal(jax.random.fold_in(_tk, 500 + 1), (1000, 32), jnp.float32)
        tbl_2 = 0.05 * jax.random.normal(jax.random.fold_in(_tk, 500 + 2), (1250, 32), jnp.float32)
        tbl_3 = 0.05 * jax.random.normal(jax.random.fold_in(_tk, 500 + 3), (1250, 32), jnp.float32)
        tbl_4 = 0.05 * jax.random.normal(jax.random.fold_in(_tk, 500 + 4), (12500, 32), jnp.float32)
        tbl_5 = 0.05 * jax.random.normal(jax.random.fold_in(_tk, 500 + 5), (1000, 32), jnp.float32)
        tbl_6 = 0.05 * jax.random.normal(jax.random.fold_in(_tk, 500 + 6), (125000, 32), jnp.float32)
        tbl_7 = 0.05 * jax.random.normal(jax.random.fold_in(_tk, 500 + 7), (125000, 32), jnp.float32)
        tbl_8 = 0.05 * jax.random.normal(jax.random.fold_in(_tk, 500 + 8), (1000, 32), jnp.float32)
        tbl_9 = 0.05 * jax.random.normal(jax.random.fold_in(_tk, 500 + 9), (125000, 32), jnp.float32)
        tbl_10 = 0.05 * jax.random.normal(jax.random.fold_in(_tk, 500 + 10), (1000, 32), jnp.float32)
        tbl_11 = 0.05 * jax.random.normal(jax.random.fold_in(_tk, 500 + 11), (125000, 32), jnp.float32)
        tbl_12 = 0.05 * jax.random.normal(jax.random.fold_in(_tk, 500 + 12), (1250, 32), jnp.float32)
        tbl_13 = 0.05 * jax.random.normal(jax.random.fold_in(_tk, 500 + 13), (125000, 32), jnp.float32)
        tbl_14 = 0.05 * jax.random.normal(jax.random.fold_in(_tk, 500 + 14), (1250, 32), jnp.float32)
        tbl_15 = 0.05 * jax.random.normal(jax.random.fold_in(_tk, 500 + 15), (125000, 32), jnp.float32)
        tbl_16 = 0.05 * jax.random.normal(jax.random.fold_in(_tk, 500 + 16), (1000, 32), jnp.float32)
        tbl_17 = 0.05 * jax.random.normal(jax.random.fold_in(_tk, 500 + 17), (1000, 32), jnp.float32)
        tbl_18 = 0.05 * jax.random.normal(jax.random.fold_in(_tk, 500 + 18), (125000, 32), jnp.float32)
        tbl_19 = 0.05 * jax.random.normal(jax.random.fold_in(_tk, 500 + 19), (12500, 32), jnp.float32)
        tbl_20 = 0.05 * jax.random.normal(jax.random.fold_in(_tk, 500 + 20), (12500, 32), jnp.float32)
        tbl_21 = 0.05 * jax.random.normal(jax.random.fold_in(_tk, 500 + 21), (1250, 32), jnp.float32)
        tbl_22 = 0.05 * jax.random.normal(jax.random.fold_in(_tk, 500 + 22), (1000, 32), jnp.float32)
        tbl_23 = 0.05 * jax.random.normal(jax.random.fold_in(_tk, 500 + 23), (1250, 32), jnp.float32)
        tbl_24 = 0.05 * jax.random.normal(jax.random.fold_in(_tk, 500 + 24), (1250, 32), jnp.float32)
        tbl_25 = 0.05 * jax.random.normal(jax.random.fold_in(_tk, 500 + 25), (1250, 32), jnp.float32)
        tbl_26 = 0.05 * jax.random.normal(jax.random.fold_in(_tk, 500 + 26), (1250, 32), jnp.float32)
        tbl_27 = 0.05 * jax.random.normal(jax.random.fold_in(_tk, 500 + 27), (1250, 32), jnp.float32)
        tbl_28 = 0.05 * jax.random.normal(jax.random.fold_in(_tk, 500 + 28), (12500, 32), jnp.float32)
        tbl_29 = 0.05 * jax.random.normal(jax.random.fold_in(_tk, 500 + 29), (12500, 32), jnp.float32)
        tbl_30 = 0.05 * jax.random.normal(jax.random.fold_in(_tk, 500 + 30), (1250, 32), jnp.float32)
        tbl_31 = 0.05 * jax.random.normal(jax.random.fold_in(_tk, 500 + 31), (1000, 32), jnp.float32)
        tbl_32 = 0.05 * jax.random.normal(jax.random.fold_in(_tk, 500 + 32), (1250, 32), jnp.float32)
        tbl_33 = 0.05 * jax.random.normal(jax.random.fold_in(_tk, 500 + 33), (1000, 32), jnp.float32)
        tbl_34 = 0.05 * jax.random.normal(jax.random.fold_in(_tk, 500 + 34), (1000, 32), jnp.float32)
        tbl_35 = 0.05 * jax.random.normal(jax.random.fold_in(_tk, 500 + 35), (12500, 32), jnp.float32)
        tbl_36 = 0.05 * jax.random.normal(jax.random.fold_in(_tk, 500 + 36), (1000, 32), jnp.float32)
        tbl_37 = 0.05 * jax.random.normal(jax.random.fold_in(_tk, 500 + 37), (1000, 32), jnp.float32)
        tbl_38 = 0.05 * jax.random.normal(jax.random.fold_in(_tk, 500 + 38), (1000, 32), jnp.float32)
        tbl_39 = 0.05 * jax.random.normal(jax.random.fold_in(_tk, 500 + 39), (1250, 32), jnp.float32)
        _rk = jax.random.fold_in(_tk, 7)
        W_top1 = 0.0354441 * jax.random.normal(jax.random.fold_in(_tk, 801), (796, 512), jnp.float32)
        W_top2 = 0.0441942 * jax.random.normal(jax.random.fold_in(_tk, 802), (512, 256), jnp.float32)
        W_top3 = 0.0625 * jax.random.normal(jax.random.fold_in(_tk, 803), (256, 1), jnp.float32)
        b_top1 = jnp.zeros((512,), jnp.float32)
        b_top2 = jnp.zeros((256,), jnp.float32)
        return (dense_ctx, ids, tbl_0, tbl_1, tbl_2, tbl_3, tbl_4, tbl_5, tbl_6, tbl_7, tbl_8, tbl_9, tbl_10, tbl_11, tbl_12, tbl_13, tbl_14, tbl_15, tbl_16, tbl_17, tbl_18, tbl_19, tbl_20, tbl_21, tbl_22, tbl_23, tbl_24, tbl_25, tbl_26, tbl_27, tbl_28, tbl_29, tbl_30, tbl_31, tbl_32, tbl_33, tbl_34, tbl_35, tbl_36, tbl_37, tbl_38, tbl_39, W_top1, b_top1, W_top2, b_top2, W_top3)
    dense_ctx, ids, tbl_0, tbl_1, tbl_2, tbl_3, tbl_4, tbl_5, tbl_6, tbl_7, tbl_8, tbl_9, tbl_10, tbl_11, tbl_12, tbl_13, tbl_14, tbl_15, tbl_16, tbl_17, tbl_18, tbl_19, tbl_20, tbl_21, tbl_22, tbl_23, tbl_24, tbl_25, tbl_26, tbl_27, tbl_28, tbl_29, tbl_30, tbl_31, tbl_32, tbl_33, tbl_34, tbl_35, tbl_36, tbl_37, tbl_38, tbl_39, W_top1, b_top1, W_top2, b_top2, W_top3 = _rec_inputs()

    def _L0_rec_setup():
        import itertools
        import jax, jax.numpy as jnp
        import numpy as np
        B, F, D = (512, 40, 32)
        P = F * (F - 1) // 2

        def _pair_indices(num_fields):
            pairs = np.array(list(itertools.combinations(range(num_fields), 2)), dtype=np.int32)
            return (pairs[:, 0], pairs[:, 1])
        key = jax.random.key(seed)
        k1, k2 = jax.random.split(key)
        x = jax.random.normal(k1, (B, F, D), dtype=jnp.float32)
        W = jax.random.normal(k2, (P, D, D), dtype=jnp.float32) * 0.05
        return {'x': x, 'W': W}
    _L0_rec_all = _L0_rec_setup()
    _L0_rec_in = {k: v for k, v in _L0_rec_all.items() if k in ('W',)}
    del _L0_rec_all
    return {'dense_ctx': dense_ctx, 'ids': ids, 'tbl_0': tbl_0, 'tbl_1': tbl_1, 'tbl_2': tbl_2, 'tbl_3': tbl_3, 'tbl_4': tbl_4, 'tbl_5': tbl_5, 'tbl_6': tbl_6, 'tbl_7': tbl_7, 'tbl_8': tbl_8, 'tbl_9': tbl_9, 'tbl_10': tbl_10, 'tbl_11': tbl_11, 'tbl_12': tbl_12, 'tbl_13': tbl_13, 'tbl_14': tbl_14, 'tbl_15': tbl_15, 'tbl_16': tbl_16, 'tbl_17': tbl_17, 'tbl_18': tbl_18, 'tbl_19': tbl_19, 'tbl_20': tbl_20, 'tbl_21': tbl_21, 'tbl_22': tbl_22, 'tbl_23': tbl_23, 'tbl_24': tbl_24, 'tbl_25': tbl_25, 'tbl_26': tbl_26, 'tbl_27': tbl_27, 'tbl_28': tbl_28, 'tbl_29': tbl_29, 'tbl_30': tbl_30, 'tbl_31': tbl_31, 'tbl_32': tbl_32, 'tbl_33': tbl_33, 'tbl_34': tbl_34, 'tbl_35': tbl_35, 'tbl_36': tbl_36, 'tbl_37': tbl_37, 'tbl_38': tbl_38, 'tbl_39': tbl_39, 'W_top1': W_top1, 'b_top1': b_top1, 'W_top2': W_top2, 'b_top2': b_top2, 'W_top3': W_top3, 'L0_rec_W': _L0_rec_in['W']}

def reference(dense_ctx, ids, tbl_0, tbl_1, tbl_2, tbl_3, tbl_4, tbl_5, tbl_6, tbl_7, tbl_8, tbl_9, tbl_10, tbl_11, tbl_12, tbl_13, tbl_14, tbl_15, tbl_16, tbl_17, tbl_18, tbl_19, tbl_20, tbl_21, tbl_22, tbl_23, tbl_24, tbl_25, tbl_26, tbl_27, tbl_28, tbl_29, tbl_30, tbl_31, tbl_32, tbl_33, tbl_34, tbl_35, tbl_36, tbl_37, tbl_38, tbl_39, W_top1, b_top1, W_top2, b_top2, W_top3, L0_rec_W):
    import jax
    import jax.numpy as jnp

    def _L0_rec_ref(x, W):
        import itertools
        import jax, jax.numpy as jnp
        import numpy as np
        B, F, D = (512, 40, 32)
        P = F * (F - 1) // 2

        def _pair_indices(num_fields):
            pairs = np.array(list(itertools.combinations(range(num_fields), 2)), dtype=np.int32)
            return (pairs[:, 0], pairs[:, 1])
        fi, fj = _pair_indices(x.shape[1])
        S = W + jnp.swapaxes(W, 1, 2)
        xi = x[:, fi, :]
        xj = x[:, fj, :]
        out = jnp.einsum('bpd,pde,bpe->bp', xi, S, xj)
        return out
    e = jnp.stack([tbl_0[ids[:, 0]], tbl_1[ids[:, 1]], tbl_2[ids[:, 2]], tbl_3[ids[:, 3]], tbl_4[ids[:, 4]], tbl_5[ids[:, 5]], tbl_6[ids[:, 6]], tbl_7[ids[:, 7]], tbl_8[ids[:, 8]], tbl_9[ids[:, 9]], tbl_10[ids[:, 10]], tbl_11[ids[:, 11]], tbl_12[ids[:, 12]], tbl_13[ids[:, 13]], tbl_14[ids[:, 14]], tbl_15[ids[:, 15]], tbl_16[ids[:, 16]], tbl_17[ids[:, 17]], tbl_18[ids[:, 18]], tbl_19[ids[:, 19]], tbl_20[ids[:, 20]], tbl_21[ids[:, 21]], tbl_22[ids[:, 22]], tbl_23[ids[:, 23]], tbl_24[ids[:, 24]], tbl_25[ids[:, 25]], tbl_26[ids[:, 26]], tbl_27[ids[:, 27]], tbl_28[ids[:, 28]], tbl_29[ids[:, 29]], tbl_30[ids[:, 30]], tbl_31[ids[:, 31]], tbl_32[ids[:, 32]], tbl_33[ids[:, 33]], tbl_34[ids[:, 34]], tbl_35[ids[:, 35]], tbl_36[ids[:, 36]], tbl_37[ids[:, 37]], tbl_38[ids[:, 38]], tbl_39[ids[:, 39]]], axis=1)
    z = _L0_rec_ref(e, L0_rec_W)
    z = z.reshape(z.shape[0], -1)
    h = jnp.concatenate([z, dense_ctx], axis=1)
    h = jnp.maximum(h @ W_top1 + b_top1, 0.0)
    h = jnp.maximum(h @ W_top2 + b_top2, 0.0)
    y = h @ W_top3
    return y

_drawn_inputs = setup_inputs


def setup_inputs(seed=0):
    import zlib

    import numpy as np

    out = dict(_drawn_inputs(seed))
    spreads = {'b_top1': (0.0, 0.1), 'b_top2': (0.0, 0.1)}
    factors = {'tbl_0': 8.0,
     'tbl_1': 8.0,
     'tbl_2': 8.0,
     'tbl_3': 7.435,
     'tbl_4': 7.811,
     'tbl_5': 7.666,
     'tbl_6': 8.0,
     'tbl_7': 7.752,
     'tbl_8': 7.629,
     'tbl_9': 7.367,
     'tbl_10': 7.732,
     'tbl_11': 8.0,
     'tbl_12': 7.426,
     'tbl_13': 7.823,
     'tbl_14': 7.858,
     'tbl_15': 8.0,
     'tbl_16': 8.0,
     'tbl_17': 7.489,
     'tbl_18': 8.0,
     'tbl_19': 8.0,
     'tbl_20': 7.614,
     'tbl_21': 8.0,
     'tbl_22': 7.884,
     'tbl_23': 7.144,
     'tbl_24': 8.0,
     'tbl_25': 8.0,
     'tbl_26': 7.58,
     'tbl_27': 8.0,
     'tbl_28': 7.849,
     'tbl_29': 7.954,
     'tbl_30': 7.918,
     'tbl_31': 7.133,
     'tbl_32': 8.0,
     'tbl_33': 7.99,
     'tbl_34': 7.835,
     'tbl_35': 7.559,
     'tbl_36': 8.0,
     'tbl_37': 8.0,
     'tbl_38': 8.0,
     'tbl_39': 7.747}
    for name, (base, spread) in spreads.items():
        noise = np.random.default_rng([zlib.crc32(name.encode()), seed]).standard_normal(out[name].shape)
        drawn = base * np.exp(spread * noise) if base else spread * noise
        out[name] = jnp.asarray(drawn.astype(out[name].dtype))
    for name, factor in factors.items():
        out[name] = (out[name] * factor).astype(out[name].dtype)
    return out
```

```python
import concourse.bass as bass
from concourse import mybir
from contextlib import ExitStack

F32 = mybir.dt.float32
F32R = mybir.dt.float32r
I32 = mybir.dt.int32
ALU = mybir.AluOpType
ACT = mybir.ActivationFunctionType
AX = mybir.AxisListType


def dlrm_tower_program(nc, ids, tables, pair_w, dense_t, w1, b1, w2, b2, w3, out):
    BATCH, FIELDS = ids.shape
    PAIRS, DIM, _ = pair_w.shape
    B = 128
    TILES = BATCH // B
    NDENSE = dense_t.shape[0]
    H1, H2 = w1.shape[1], w2.shape[1]
    M1, M2 = H1 // 128, H2 // 128

    row_start = [0]
    for i in range(FIELDS - 1):
        row_start.append(row_start[-1] + FIELDS - 1 - i)

    CH = 32
    BANK = 16
    CHUNKS = -(-PAIRS // CH)
    GRP = 128
    CPG = GRP // CH
    FULL = PAIRS // GRP
    REST = PAIRS - FULL * GRP
    GROUPS = FULL + 1
    E_DVE = 15
    SUMS = DIM - E_DVE + 1
    UNIT = 8
    UNITS = FIELDS // UNIT
    BATCHF = 4
    BATCHES = FIELDS // BATCHF

    def pieces(lo, hi, cut):
        at = lo
        while at < hi:
            i = max(r for r in range(FIELDS - 1) if row_start[r] <= at)
            end = min(hi, row_start[i + 1], (at // cut + 1) * cut)
            yield i, at, end
            at = end

    def chunk(c):
        return c * CH, min((c + 1) * CH, PAIRS)

    UNIT_SLOT = [0, 2, 6, 10, 14]
    BATCH_SLOT = [0, 1, 4, 5, 8, 9, 12, 13, 16, 17]
    TOP1_SLOT = 5
    TOP2_SLOT = 20
    TOP3_SLOT = 24
    part_len = [SUMS // 4 + (k < SUMS % 4) for k in range(4)]
    part_at = [sum(part_len[:k]) for k in range(5)]
    K1 = FULL + 1
    top1_steps = [(m, k) for m in range(M1) for k in range(K1)]
    top2_steps = [(m, k) for m in range(M2) for k in range(M1)]

    QUARTERS = 128 // DIM
    QP = PAIRS // QUARTERS
    PIECE = 39
    NPIECE = QP // PIECE
    PC = PIECE * DIM

    with ExitStack() as ctx:
        def sb(name, shape, dt=F32):
            return ctx.enter_context(nc.sbuf_tensor(name, shape, dt))

        def ps(name, shape):
            return ctx.enter_context(nc.psum_tensor(name, shape, F32))

        def sem(name):
            return ctx.enter_context(nc.semaphore(name))

        s_stack = sb("s_stack", [128, PAIRS * DIM], F32R)
        products = sb("products", [128, 2, GRP * DIM])
        products_rest = sb("products_rest", [128, REST * DIM])
        x_rows = [sb(f"x_rows{h}", [128, FIELDS * DIM]) for h in range(2)]
        x_split = sb("x_split", [128, 2, UNIT, 4, DIM], F32R)
        x_stack = sb("x_stack", [128, FIELDS, B], F32R)
        ids_sb = [sb(f"ids_sb{h}", [128, FIELDS], I32) for h in range(2)]
        partial = sb("partial", [128, 2, GRP])
        partial_rest = sb("partial_rest", [128, REST])
        z_t = sb("z_t", [128, 2, K1, B])
        h1_t = sb("h1_t", [128, M1, B])
        h2_t = sb("h2_t", [128, M2, B])
        y_row = sb("y_row", [1, 2, B])
        w1_sb = sb("w1_sb", [128, K1, H1])
        w2_sb = sb("w2_sb", [128, M1, H2])
        w3_sb = sb("w3_sb", [128, M2])
        b1_sb = sb("b1_sb", [128, M1])
        b2_sb = sb("b2_sb", [128, M2])
        ident = sb("ident", [128, 128])
        ident_r = sb("ident_r", [128, 128], F32R)

        room = products[:, :, :].rearrange("p a n -> p (a n)")
        w_in = [room[:, k * PC:(k + 1) * PC] for k in range(2)]
        s_sum = room[:, 2 * PC:3 * PC]
        s_hi = [room[:, (3 + k) * PC:(4 + k) * PC].bitcast(F32R) for k in range(2)]
        s_lo = room[:, 5 * PC:6 * PC].bitcast(F32R)

        prod_ps = [ps(f"prod_ps{k}", [128, CH * DIM]) for k in range(2)]
        xt_ps = ps("xt_ps", [128, BATCHF, B])
        z_ps = [ps(f"z_ps{k}", [128, 4, B]) for k in range(2)]
        top_ps = ps("top_ps", [128, 4, B])

        ids_loaded = [sem(f"ids_loaded{h}") for h in range(2)]
        x_gathered = [sem(f"x_gathered{h}") for h in range(2)]
        dense_loaded = [sem(f"dense_loaded{h}") for h in range(2)]
        w_loaded = [sem(f"w_loaded{k}") for k in range(2)]
        w_turned = sem("w_turned")
        s_summed = sem("s_summed")
        s_hi_made = sem("s_hi_made")
        s_lo_made = sem("s_lo_made")
        s_placed = sem("s_placed")
        s_placed_hi = [sem(f"s_placed_hi{k}") for k in range(2)]
        gathers_begun = sem("gathers_begun")
        ids_begun = sem("ids_begun")
        weights_loaded = sem("weights_loaded")
        ident_made = sem("ident_made")
        ident_r_made = sem("ident_r_made")
        hi_made = sem("hi_made")
        lo_made = sem("lo_made")
        split_made = sem("split_made")
        xt_made = sem("xt_made")
        x_stacked = sem("x_stacked")
        t_made = sem("t_made")
        multiplied = sem("multiplied")
        part_summed = sem("part_summed")
        z_summed = sem("z_summed")
        z_stored = sem("z_stored")
        l1_summed = sem("l1_summed")
        h1_stored = sem("h1_stored")
        l2_summed = sem("l2_summed")
        h2_stored = sem("h2_stored")
        y_summed = sem("y_summed")
        y_stored = sem("y_stored")
        y_written = [sem(f"y_written{h}") for h in range(2)]

        def after(it, h, per_tile, n):
            return it * (2 * per_tile) + (h * per_tile + n)

        def wait(engine, semaphore, value):
            if not isinstance(value, int) or value > 0:
                engine.wait_ge(semaphore, value)

        block = ctx.enter_context(nc.Block())

        @block.sync
        def _(sp):
            def place_lo(sp, k):
                sp.wait_ge(s_lo_made, k + 1)
                for q in range(QUARTERS):
                    at = (q * QP + k * PIECE) * DIM
                    for r in (2, 3):
                        sp.dma_start(s_stack[r * DIM:(r + 1) * DIM, at:at + PC].bitcast(F32),
                                     s_lo[q * DIM:(q + 1) * DIM, :].bitcast(F32)).then_inc(s_placed, 16)

            for h in range(2):
                sp.dma_start(ids_sb[h][:, :], ids[h * B:(h + 1) * B, :]).then_inc(ids_loaded[h], 16)
            w_view = pair_w.rearrange("(q p) d e -> q d p e", q=QUARTERS)
            for k in range(NPIECE):
                if k >= 2:
                    sp.wait_ge(s_summed, k - 1)
                for q in range(QUARTERS):
                    sp.dma_start(
                        w_in[k % 2][q * DIM:(q + 1) * DIM, :].rearrange("d (p e) -> d p e", e=DIM),
                        w_view[q, :, k * PIECE:(k + 1) * PIECE, :]).then_inc(w_loaded[k % 2], 16)
                if k >= 1:
                    place_lo(sp, k - 1)
            place_lo(sp, NPIECE - 1)

            def tile(it, h):
                row = it * (2 * B) + h * B
                if not isinstance(it, int):
                    row = sp.snap(row)
                    sp.wait_ge(x_gathered[h], it * (16 * FIELDS))
                    sp.sem_inc(ids_begun, 1)
                    sp.dma_start(ids_sb[h][:, :], ids[bass.ds(row, B), :]).then_inc(ids_loaded[h], 16)
                if not isinstance(it, int):
                    sp.wait_ge(l1_summed, after(it, h, M1, -M1))
                    sp.sem_inc(ids_begun, 1)
                sp.dma_start(z_t[REST:REST + NDENSE, h, FULL, :],
                             dense_t[:, bass.ds(row, B)]).then_inc(dense_loaded[h], 16)

            tile(0, 0)
            tile(0, 1)
            with sp.Fori(1, TILES // 2) as it:
                tile(it, 0)
                tile(it, 1)

        @block.gpsimd
        def _(pool):
            nc.gpsimd.memset(ident[:, :], 1.0).then_inc(ident_made, 1)
            pool.wait_ge(ident_made, 1)
            nc.gpsimd.affine_select(out=ident[:, :], in_=ident[:, :], compare_op=ALU.is_equal, fill=0.0,
                                    base=0, pattern=[[1, 128]], channel_multiplier=-1).then_inc(ident_made, 1)

            def tile(it, h):
                wait(pool, multiplied, after(it, h, CHUNKS, -CHUNKS))
                pool.wait_ge(ids_loaded[h], (it + 1) * 16)
                pool.sem_inc(gathers_begun, 1)
                for f in range(FIELDS):
                    pool.indirect_dma_start(
                        x_rows[h][:, f * DIM:(f + 1) * DIM], None, tables[f],
                        bass.IndirectOffsetOnAxis(ap=ids_sb[h][:, f:f + 1], axis=0)).then_inc(x_gathered[h], 16)

            tile(0, 0)
            tile(0, 1)
            with pool.Fori(1, TILES // 2) as it:
                tile(it, 0)
                tile(it, 1)

        @block.scalar
        def _(act):
            act.dma_start(w1_sb[:, 0:FULL, :],
                          w1[0:FULL * GRP, :].rearrange("(k p) n -> p k n", p=128)).then_inc(weights_loaded, 16)
            act.dma_start(w1_sb[0:REST + NDENSE, FULL, :], w1[FULL * GRP:, :]).then_inc(weights_loaded, 16)
            act.dma_start(w2_sb[:, :, :], w2.rearrange("(k p) n -> p k n", p=128)).then_inc(weights_loaded, 16)
            act.dma_start(w3_sb[:, :], w3[:, :]).then_inc(weights_loaded, 16)
            act.dma_start(b1_sb[:, :], b1[:, :]).then_inc(weights_loaded, 16)
            act.dma_start(b2_sb[:, :], b2[:, :]).then_inc(weights_loaded, 16)
            act.wait_ge(ident_made, 2)
            nc.scalar.activation(ident_r[:, :], ident[:, :], ACT.Copy).then_inc(ident_r_made, 1)
            for k in range(NPIECE):
                act.wait_ge(s_summed, k + 1)
                if k >= 2:
                    act.wait_ge(s_placed_hi[k % 2], (k // 2) * 16 * 2 * QUARTERS)
                    act.wait_ge(s_lo_made, k - 1)
                nc.scalar.activation(s_hi[k % 2], s_sum, ACT.Copy).then_inc(s_hi_made, 1)
                act.wait_ge(s_hi_made, k + 1)
                for q in range(QUARTERS):
                    at = (q * QP + k * PIECE) * DIM
                    for r in (0, 1):
                        act.dma_start(s_stack[r * DIM:(r + 1) * DIM, at:at + PC].bitcast(F32),
                                      s_hi[k % 2][q * DIM:(q + 1) * DIM, :].bitcast(F32)).then_inc(s_placed_hi[k % 2], 16)

            def field_view(h, u):
                return x_rows[h][:, u * UNIT * DIM:(u + 1) * UNIT * DIM].rearrange("p (f d) -> p f d", d=DIM)

            def split_unit(it, h, u):
                s = (UNITS * h + u) % 2
                if u == 0:
                    act.wait_ge(x_gathered[h], (it + 1) * (16 * FIELDS))
                wait(act, xt_made, after(it, h, BATCHES, 2 * (u - 1)))
                nc.scalar.activation(x_split[:, s, :, 0::2, :],
                                     field_view(h, u).unsqueeze(2).to_broadcast([128, UNIT, 2, DIM]),
                                     ACT.Copy).then_inc(hi_made, 1)
                act.wait_ge(lo_made, after(it, h, UNITS, u + 1))
                nc.scalar.activation(x_split[:, s, :, 3, :], x_split[:, s, :, 1, :],
                                     ACT.Copy).then_inc(split_made, 1)

            def stack_batch(it, h, b):
                act.wait_ge(xt_made, after(it, h, BATCHES, b + 1))
                nc.scalar.activation(x_stack[:, b * BATCHF:(b + 1) * BATCHF, :], xt_ps[:, :, :],
                                     ACT.Copy).then_inc(x_stacked, 1)

            def store_z(it, h, g):
                act.wait_ge(z_summed, after(it, h, GROUPS, g + 1))
                if g == 0:
                    wait(act, l1_summed, after(it, h, M1, -M1))
                if g < FULL:
                    nc.scalar.activation(z_t[:, h, g, :], z_ps[g % 2][:, 0, :], ACT.Copy).then_inc(z_stored, 1)
                else:
                    nc.scalar.activation(z_t[0:REST, h, g, :], z_ps[FULL % 2][0:REST, 0, :], ACT.Copy).then_inc(z_stored, 1)

            def store_h1(it, h, m):
                act.wait_ge(l1_summed, after(it, h, M1, M1))
                nc.scalar.activation(h1_t[:, m, :], top_ps[:, m, :], ACT.Relu,
                                     bias=b1_sb[:, m:m + 1]).then_inc(h1_stored, 1)

            def store_h2(it, h, m):
                act.wait_ge(l2_summed, after(it, h, M2, M2))
                nc.scalar.activation(h2_t[:, m, :], top_ps[:, m, :], ACT.Relu,
                                     bias=b2_sb[:, m:m + 1]).then_inc(h2_stored, 1)

            def store_y(it, h, row):
                act.wait_ge(y_summed, after(it, h, 1, 1))
                wait(act, y_written[h], it * 16)
                nc.scalar.activation(y_row[0:1, h, :], top_ps[0:1, 2, :], ACT.Copy).then_inc(y_stored, 1)
                act.wait_ge(y_stored, after(it, h, 1, 1))
                act.dma_start(out[bass.ds(row, B), :].rearrange("b o -> o b"),
                              y_row[0:1, h, :]).then_inc(y_written[h], 16)

            top1_end = TOP1_SLOT + (K1 * M1 - 1) // 2
            top2_end = TOP2_SLOT + (M1 * M2 - 1) // 2

            def tile(it, h, before):
                for s in range(CHUNKS):
                    if s in UNIT_SLOT:
                        split_unit(it, h, UNIT_SLOT.index(s))
                    if s in BATCH_SLOT:
                        stack_batch(it, h, BATCH_SLOT.index(s))
                    if before and s == 3:
                        store_z(*before[:2], FULL - 1)
                        store_z(*before[:2], FULL)
                    if s >= 8 and s % 4 == 0:
                        store_z(it, h, s // 4 - 2)
                    if before:
                        if s == top1_end:
                            act.wait_ge(weights_loaded, 16 * 6)
                            for m in range(M1):
                                store_h1(*before[:2], m)
                        if s == top2_end:
                            for m in range(M2):
                                store_h2(*before[:2], m)
                        if s == TOP3_SLOT:
                            store_y(*before)

            tile(0, 0, None)
            tile(0, 1, (0, 0, 0))
            with act.Fori(1, TILES // 2) as it:
                tile(it, 0, (it - 1, 1, it * (2 * B) - B))
                tile(it, 1, (it, 0, it * (2 * B)))
            last = TILES // 2 - 1
            store_z(last, 1, FULL - 1)
            store_z(last, 1, FULL)
            for m in range(M1):
                store_h1(last, 1, m)
            for m in range(M2):
                store_h2(last, 1, m)
            store_y(last, 1, BATCH - B)
            for h in range(2):
                act.wait_ge(y_written[h], 16 * (TILES // 2))

        @block.vector
        def _(dve):
            for k in range(NPIECE):
                dve.wait_ge(w_loaded[k % 2], 16 * QUARTERS * (k // 2 + 1))
                if k >= 1:
                    dve.wait_ge(s_hi_made, k)
                    dve.wait_ge(s_lo_made, k)
                nc.vector.transpose(s_sum, w_in[k % 2]).then_inc(w_turned, 1)
                dve.wait_ge(w_turned, k + 1)
                nc.vector.tensor_tensor(s_sum, s_sum, w_in[k % 2], ALU.add).then_inc(s_summed, 1)
                dve.wait_ge(s_summed, k + 1)
                dve.wait_ge(s_hi_made, k + 1)
                if k >= 1:
                    dve.wait_ge(s_placed, k * 16 * 2 * QUARTERS)
                nc.vector.tensor_tensor(s_lo, s_sum, s_hi[k % 2].bitcast(F32), ALU.subtract).then_inc(s_lo_made, 1)

            def low_part(it, h, u):
                s = (UNITS * h + u) % 2
                if u == 0:
                    dve.wait_ge(x_gathered[h], (it + 1) * (16 * FIELDS))
                dve.wait_ge(hi_made, after(it, h, UNITS, u + 1))
                nc.vector.tensor_tensor(
                    x_split[:, s, :, 1, :],
                    x_rows[h][:, u * UNIT * DIM:(u + 1) * UNIT * DIM].rearrange("p (f d) -> p f d", d=DIM),
                    x_split[:, s, :, 0, :].bitcast(F32), ALU.subtract).then_inc(lo_made, 1)

            def multiply(it, h, c):
                lo, hi = chunk(c)
                g = c // CPG
                if c % CPG == 0 and g < FULL:
                    wait(dve, z_summed, after(it, h, GROUPS, g - 1 if g >= 2 else g - 2))
                if g == FULL:
                    wait(dve, z_summed, after(it, h, GROUPS, 0))
                dve.wait_ge(t_made, after(it, h, CHUNKS, c + 1))
                for i, a, b in pieces(lo, hi, CH):
                    j = i + 1 + a - row_start[i]
                    if g < FULL:
                        at = (a - g * GRP) * DIM
                        dst = products[:, g % 2, at:at + (b - a) * DIM]
                    else:
                        dst = products_rest[:, (a - lo) * DIM:(b - lo) * DIM]
                    last = nc.vector.tensor_tensor(
                        dst, prod_ps[(CHUNKS * h + c) % 2][:, (a - lo) * DIM:(b - lo) * DIM],
                        x_rows[h][:, j * DIM:(j + b - a) * DIM], ALU.mult)
                last.then_inc(multiplied, 1)

            def sum_part(it, h, g):
                dve.wait_ge(multiplied, after(it, h, CHUNKS, min(CPG * (g + 1), CHUNKS)))
                if g < FULL:
                    wait(dve, z_summed, after(it, h, GROUPS, g - 1 if g >= 2 else g - 2))
                    nc.vector.tensor_reduce(
                        partial[:, g % 2, :],
                        products[:, g % 2, :].rearrange("p (n e) -> p n e", e=DIM)[:, :, 0:E_DVE],
                        AX.X, ALU.add).then_inc(part_summed, 1)
                else:
                    nc.vector.tensor_reduce(
                        partial_rest[:, :], products_rest[:, :].rearrange("p (n e) -> p n e", e=DIM),
                        AX.X, ALU.add).then_inc(part_summed, 1)

            def tile(it, h, before):
                low_part(it, h, 0)
                if before:
                    sum_part(*before, FULL - 1)
                    sum_part(*before, FULL)
                for c in range(CHUNKS):
                    multiply(it, h, c)
                    if c in UNIT_SLOT[1:]:
                        low_part(it, h, UNIT_SLOT.index(c))
                    if c >= CPG and c % CPG == 0 and c // CPG <= FULL - 1:
                        sum_part(it, h, c // CPG - 1)

            tile(0, 0, None)
            tile(0, 1, (0, 0))
            with dve.Fori(1, TILES // 2) as it:
                tile(it, 0, (it - 1, 1))
                tile(it, 1, (it, 0))
            sum_part(TILES // 2 - 1, 1, FULL - 1)
            sum_part(TILES // 2 - 1, 1, FULL)

        @block.tensor
        def _(pe):
            def turn_batch(it, h, b):
                u = b * BATCHF // UNIT
                s = (UNITS * h + u) % 2
                pe.wait_ge(split_made, after(it, h, UNITS, u + 1))
                wait(pe, x_stacked, after(it, h, BATCHES, b))
                for k in range(BATCHF):
                    f = (b * BATCHF + k) % UNIT
                    last = nc.tensor.matmul(xt_ps[:, k, :],
                                            x_split[:, s, f, :, :].rearrange("p r d -> p (r d)"),
                                            ident_r[:, :], start=True, stop=True)
                last.then_inc(xt_made, 1)

            def row_products(it, h, c):
                lo, hi = chunk(c)
                wait(pe, multiplied, after(it, h, CHUNKS, c - 1))
                waited = -1
                for i, a, b in pieces(lo, hi, BANK):
                    if i // BATCHF > waited:
                        waited = i // BATCHF
                        pe.wait_ge(x_stacked, after(it, h, BATCHES, waited + 1))
                    last = nc.tensor.matmul(
                        prod_ps[(CHUNKS * h + c) % 2][:, (a - lo) * DIM:(b - lo) * DIM],
                        x_stack[:, i, :], s_stack[:, a * DIM:b * DIM], start=True, stop=True)
                last.then_inc(t_made, 1)

            def sum_group(it, h, g, part):
                if part == 0:
                    pe.wait_ge(multiplied, after(it, h, CHUNKS, CPG * (g + 1)))
                    wait(pe, z_stored, after(it, h, GROUPS, g - 1 if g >= 2 else -g))
                p = products[:, g % 2, :].rearrange("p (n e) -> p n e", e=DIM)
                for n in range(part_at[part], part_at[part + 1]):
                    if n < SUMS - 1:
                        lhs = p[:, :, E_DVE + n]
                    else:
                        pe.wait_ge(part_summed, after(it, h, GROUPS, g + 1))
                        lhs = partial[:, g % 2, :]
                    last = nc.tensor.matmul(z_ps[g % 2][:, 0, :], lhs, ident[:, :],
                                            start=(n == 0), stop=(n == SUMS - 1))
                if part == 3:
                    last.then_inc(z_summed, 1)

            def sum_rest(it, h):
                pe.wait_ge(part_summed, after(it, h, GROUPS, GROUPS))
                pe.wait_ge(z_stored, after(it, h, GROUPS, FULL - 1))
                nc.tensor.matmul(z_ps[FULL % 2][0:REST, 0, :], partial_rest[:, :], ident[:, :],
                                 start=True, stop=True).then_inc(z_summed, 1)

            def layer1(it, h, step):
                m, k = top1_steps[step]
                if step == 0:
                    pe.wait_ge(weights_loaded, 16 * 6)
                    pe.wait_ge(dense_loaded[h], (it + 1) * 16)
                    pe.wait_ge(z_stored, after(it, h, GROUPS, GROUPS))
                    wait(pe, y_stored, after(it, h, 1, 0))
                rows = 128 if k < FULL else REST + NDENSE
                last = nc.tensor.matmul(top_ps[:, m, :], w1_sb[0:rows, k, m * 128:(m + 1) * 128],
                                        z_t[0:rows, h, k, :], start=(k == 0), stop=(k == K1 - 1))
                if k == K1 - 1:
                    last.then_inc(l1_summed, 1)

            def layer2(it, h, step):
                m, k = top2_steps[step]
                if step == 0:
                    pe.wait_ge(h1_stored, after(it, h, M1, M1))
                last = nc.tensor.matmul(top_ps[:, m, :], w2_sb[:, k, m * 128:(m + 1) * 128],
                                        h1_t[:, k, :], start=(k == 0), stop=(k == M1 - 1))
                if k == M1 - 1:
                    last.then_inc(l2_summed, 1)

            def layer3(it, h):
                pe.wait_ge(h2_stored, after(it, h, M2, M2))
                for k in range(M2):
                    last = nc.tensor.matmul(top_ps[0:1, 2, :], w3_sb[:, k:k + 1], h2_t[:, k, :],
                                            start=(k == 0), stop=(k == M2 - 1))
                last.then_inc(y_summed, 1)

            def tile(it, h, before):
                for s in range(CHUNKS):
                    if s in BATCH_SLOT:
                        turn_batch(it, h, BATCH_SLOT.index(s))
                    row_products(it, h, s)
                    if before and s < 4:
                        sum_group(*before, FULL - 1, s)
                    if before and s == 3:
                        sum_rest(*before)
                    if s >= 5:
                        sum_group(it, h, (s - 5) // 4, (s - 5) % 4)
                    if before:
                        for n in range(2 * (s - TOP1_SLOT), 2 * (s - TOP1_SLOT) + 2):
                            if 0 <= n < len(top1_steps):
                                layer1(*before, n)
                        for n in range(2 * (s - TOP2_SLOT), 2 * (s - TOP2_SLOT) + 2):
                            if 0 <= n < len(top2_steps):
                                layer2(*before, n)
                        if s == TOP3_SLOT:
                            layer3(*before)

            pe.wait_ge(ident_made, 2)
            pe.wait_ge(ident_r_made, 1)
            pe.wait_ge(s_placed, NPIECE * 16 * 2 * QUARTERS)
            pe.wait_ge(s_placed_hi[0], -(-NPIECE // 2) * 16 * 2 * QUARTERS)
            pe.wait_ge(s_placed_hi[1], (NPIECE // 2) * 16 * 2 * QUARTERS)
            tile(0, 0, None)
            tile(0, 1, (0, 0))
            with pe.Fori(1, TILES // 2) as it:
                tile(it, 0, (it - 1, 1))
                tile(it, 1, (it, 0))
            last_tile = (TILES // 2 - 1, 1)
            for part in range(4):
                sum_group(*last_tile, FULL - 1, part)
            sum_rest(*last_tile)
            for n in range(len(top1_steps)):
                layer1(*last_tile, n)
            for n in range(len(top2_steps)):
                layer2(*last_tile, n)
            layer3(*last_tile)


N_TABLES = 40


def kernel(**inputs):
    import numpy as _np
    import concourse.bacc as _bacc
    from concourse import mybir as _mybir
    from concourse.bass_utils import run_bass_kernel_spmd as _run

    nc = _bacc.Bacc("TRN2", target_bir_lowering=False, num_devices=1)
    arrays = {}

    def dram(name, a):
        a = _np.ascontiguousarray(a)
        arrays[name] = a
        return nc.dram_tensor(name, a.shape, _mybir.dt.from_np(a.dtype), kind="ExternalInput").ap()

    ids = dram("ids_dram", inputs["ids"])
    tables = [dram(f"tbl_{f}_dram", inputs[f"tbl_{f}"]) for f in range(N_TABLES)]
    pair_w = dram("pair_w_dram", inputs["L0_rec_W"])
    dense_t = dram("dense_t_dram", _np.asarray(inputs["dense_ctx"]).T)
    w1, w2 = (dram(f"{n}_dram", inputs[n]) for n in ("W_top1", "W_top2"))
    b1, b2, w3 = (dram(f"{n}_dram", _np.asarray(inputs[n]).reshape(-1, 128).T)
                  for n in ("b_top1", "b_top2", "W_top3"))
    out = nc.dram_tensor("out_0_dram", (ids.shape[0], 1), _mybir.dt.float32, kind="ExternalOutput").ap()
    dlrm_tower_program(nc, ids, tables, pair_w, dense_t, w1, b1, w2, b2, w3, out)
    r = _run(nc, [arrays], core_ids=[0])
    return r.results[0]["out_0_dram"]
```

```python
import concourse.bass as bass
from concourse import mybir
from contextlib import ExitStack

F32 = mybir.dt.float32
F32R = mybir.dt.float32r
I32 = mybir.dt.int32
ALU = mybir.AluOpType
ACT = mybir.ActivationFunctionType
AX = mybir.AxisListType


def natural(i, j, fields):
    return i * fields - i * (i + 1) // 2 + j - i - 1


def pair_chunks(fields, most, rows):
    wide, half, tri = most // rows, rows * rows, rows * (rows - 1) // 2
    chunks, mixed = [], []
    for u in range(0, fields, 2 * rows):
        for i0 in (u, u + rows):
            for j0 in range(i0 + rows, fields - wide + 1, wide):
                chunks.append([("rect", i0, j0, wide, 0)])
        chunks.append([("rect", u, fields - rows, rows, 0),
                       ("tri", u, None, None, half), ("tri", u + rows, None, None, half + tri)])
        mixed.append(len(chunks) - 1)
    return chunks, mixed


def strips(chunk, rows):
    for kind, i0, j0, width, at in chunk:
        for r in range(rows):
            if kind == "rect":
                yield i0 + r, j0, width, at + r * width
            elif r < rows - 1:
                yield i0 + r, i0 + r + 1, rows - 1 - r, at
                at += rows - 1 - r


def dlrm_tower_program(nc, ids, tables, pair_w, dense_t, w1, b1, w2, b2, w3, out):
    BATCH, FIELDS = ids.shape
    PAIRS, DIM, _ = pair_w.shape
    B = 128
    TILES = BATCH // B
    PAIRS_OF_TILES = TILES // 2
    NDENSE = dense_t.shape[0]
    H1, H2 = w1.shape[1], w2.shape[1]
    M1, M2 = H1 // 128, H2 // 128

    CH = 32
    ROWS = 4
    UNIT = 2 * ROWS
    UNITS = FIELDS // UNIT
    WIDE = CH // ROWS
    TRI = ROWS * (ROWS - 1) // 2
    chunks, mixed = pair_chunks(FIELDS, CH, ROWS)
    CHUNKS = len(chunks)
    size = [sum(n for _, _, n, _ in strips(chunk, ROWS)) for chunk in chunks]
    assert sum(size) == PAIRS

    def units_read(c):
        return {f // UNIT for _, j, n, _ in strips(chunks[c], ROWS) for f in range(j, j + n)}

    CPG = 4
    FULL = CHUNKS // CPG
    GROUPS = FULL + 1
    group_size = [sum(size[g * CPG:(g + 1) * CPG]) for g in range(GROUPS)]
    GRP = max(group_size)
    REST = group_size[FULL]
    E_DVE = 16
    SUMS = DIM - E_DVE + 1
    RED = 2
    PARTS = FULL * CPG // RED + 1

    def place(c):
        return sum(size[c // CPG * CPG:c])

    K1 = GROUPS
    k1_rows = group_size[:FULL] + [REST + NDENSE]
    top1_steps = [(m, k) for m in range(M1) for k in range(K1)]
    top2_steps = [(m, k) for m in range(M2) for k in range(M1)]

    RECT_AT = [8, 12, 24, 28]
    TRI_AT = [[0, 3, 16], [5, 17, 19]]

    SPLIT_SLOT = {0: 1, 5: 2, 10: 3, 15: 4}
    TURN_SLOT = {4: 1, 9: 2, 14: 3, 19: 4}
    NEXT_SPLIT_SLOT = 19
    NEXT_TURN_SLOT = 23
    SUM_PARTS = CPG - 1
    part_len = [SUMS // SUM_PARTS + (k < SUMS % SUM_PARTS) for k in range(SUM_PARTS)]
    part_at = [sum(part_len[:k]) for k in range(SUM_PARTS + 1)]

    def sums_in(s):
        if s < SUM_PARTS:
            return 1, FULL - 1, s
        g, part = divmod(s - CPG - 1, CPG)
        return None if s < CPG or part == SUM_PARTS else (0, g, part)

    def plan_layers():
        load = []
        for s in range(CHUNKS):
            matmuls = 4 if len(chunks[s]) == 1 else 7 if s < CHUNKS - 1 else 10
            turns = 4 * (s in TURN_SLOT or s == NEXT_TURN_SLOT)
            sums = 2 * (part_len[sums_in(s)[2]] if sums_in(s) else 0) + 2 * (s == CPG - 2)
            load.append(matmuls + turns + sums)
        steps = len(top1_steps) + len(top2_steps)
        mean = (sum(load) + 2 * (steps + M2)) / CHUNKS
        slots, done, first2 = [], 0, 0
        for s in range(CHUNKS):
            slots.append([])
            room = (s + 1) * mean - sum(load[:s + 1])
            while s >= CPG and done < steps and 2 * (done + 1) <= room:
                if done == len(top1_steps) and s < first2:
                    break
                slots[s].append(done)
                done += 1
                first2 = s + 2 if done == len(top1_steps) else first2
        slots[CHUNKS - 2] += range(done, steps)
        return slots

    layer_slots = plan_layers()
    LAYER1_END = next(s for s in range(CHUNKS) if len(top1_steps) - 1 in layer_slots[s])
    LAYER2_END = next(s for s in range(CHUNKS) if len(top1_steps) + len(top2_steps) - 1 in layer_slots[s])
    LAYER3_SLOT = CHUNKS - 1

    QUARTERS = 128 // DIM
    QP = PAIRS // QUARTERS
    PIECE = 15
    NPIECE = QP // PIECE
    PC = PIECE * DIM
    LOADS = [0, 1, 3, 7, NPIECE]
    RING = 3
    FIRST_TURN = 8

    with ExitStack() as ctx:
        def sb(name, shape, dt=F32):
            return ctx.enter_context(nc.sbuf_tensor(name, shape, dt))

        def ps(name, shape):
            return ctx.enter_context(nc.psum_tensor(name, shape, F32))

        def sem(name):
            return ctx.enter_context(nc.semaphore(name))

        s_stack = sb("s_stack", [128, PAIRS * DIM], F32R)
        products = sb("products", [128, 2, GRP * DIM])
        products_rest = sb("products_rest", [128, REST * DIM])
        x_rows = [sb(f"x_rows{h}", [128, FIELDS * DIM]) for h in range(2)]
        x_split = sb("x_split", [128, 2, UNIT, 2, DIM], F32R)
        x_stack = sb("x_stack", [128, FIELDS, B], F32R)
        ids_sb = [sb(f"ids_sb{h}", [128, FIELDS], I32) for h in range(2)]
        partial = sb("partial", [128, 2, GRP])
        partial_rest = sb("partial_rest", [128, REST])
        z_t = sb("z_t", [128, 2, K1, B])
        h1_t = sb("h1_t", [128, M1, B])
        h2_t = sb("h2_t", [128, M2, B])
        y_row = sb("y_row", [1, 2, B])
        w1_sb = sb("w1_sb", [128, K1, H1])
        w2_sb = sb("w2_sb", [128, M1, H2])
        w3_sb = sb("w3_sb", [128, M2])
        b1_sb = sb("b1_sb", [128, M1])
        b2_sb = sb("b2_sb", [128, M2])
        ident = sb("ident", [128, 128])
        ident_r = sb("ident_r", [128, 128], F32R)

        room = products[:, :, :].rearrange("p a n -> p (a n)")
        w_in = room[:, 0:QP * DIM]
        s_sum = [room[:, QP * DIM + k * PC:QP * DIM + (k + 1) * PC] for k in range(RING)]
        room_r = x_stack[:, UNIT:, :].rearrange("p f b -> p (f b)")
        base = QUARTERS * 2 * 128
        spread = room_r[:, 0:base].rearrange("p (q l m) -> p q l m", q=QUARTERS, l=2)
        s_hi = [room_r[:, base + k * PC:base + (k + 1) * PC] for k in range(RING)]
        s_lo = [room_r[:, base + (RING + k) * PC:base + (RING + k + 1) * PC] for k in range(RING)]

        prod_ps = [ps(f"prod_ps{k}", [128, CH * DIM]) for k in range(2)]
        other_ps = [ps(f"other_ps{k}", [128, 2, 4, B]) for k in range(2)]
        xt_ps, top_ps = other_ps[0][:, 0], other_ps[0][:, 1]
        z_ps = [other_ps[1][:, k] for k in range(2)]

        ids_loaded = [sem(f"ids_loaded{h}") for h in range(2)]
        x_gathered = [[sem(f"x_gathered{h}_{u}") for u in range(UNITS)] for h in range(2)]
        dense_loaded = [sem(f"dense_loaded{h}") for h in range(2)]
        w_loaded = [sem(f"w_loaded{k}") for k in range(len(LOADS) - 1)]
        w_turned = sem("w_turned")
        s_summed = sem("s_summed")
        s_hi_made = sem("s_hi_made")
        s_lo_made = sem("s_lo_made")
        spread_zeroed = sem("spread_zeroed")
        spread_made = sem("spread_made")
        s_spread = [sem(f"s_spread{k}") for k in range(2)]
        s_placed = sem("s_placed")
        s_placed_act = sem("s_placed_act")
        s_placed_dve = sem("s_placed_dve")
        pool_steps = sem("pool_steps")
        sp_steps = sem("sp_steps")
        weights_loaded = sem("weights_loaded")
        ident_made = sem("ident_made")
        ident_r_made = sem("ident_r_made")
        hi_made = sem("hi_made")
        lo_made = sem("lo_made")
        xt_made = sem("xt_made")
        x_stacked = sem("x_stacked")
        t_made = sem("t_made")
        multiplied = sem("multiplied")
        part_summed = sem("part_summed")
        z_summed = sem("z_summed")
        z_stored = sem("z_stored")
        l1_summed = sem("l1_summed")
        h1_stored = sem("h1_stored")
        l2_summed = sem("l2_summed")
        h2_stored = sem("h2_stored")
        y_summed = sem("y_summed")
        y_stored = sem("y_stored")
        y_written = [sem(f"y_written{h}") for h in range(2)]

        def after(it, h, per_tile, n):
            return it * (2 * per_tile) + (h * per_tile + n)

        def wait(engine, semaphore, value):
            if not isinstance(value, int) or value > 0:
                engine.wait_ge(semaphore, value)

        def stack_part(half, k):
            at = s_stack[:, :].rearrange("p (q n) -> p q n", q=QUARTERS)
            return at[:, 2 * half:2 * half + 2, k * PC:(k + 1) * PC]

        def spread_part(half, k):
            if k % 2 == 0:
                return prod_ps[half][:, :].rearrange("p (q n) -> p q n", q=2)[:, :, 0:PC]
            return other_ps[half][:, :, :, :].rearrange("p q a b -> p q (a b)")[:, :, 0:PC]

        block = ctx.enter_context(nc.Block())

        @block.sync
        def _(sp):
            sp.dma_start(ids_sb[0][:, :], ids[0:B, :]).then_inc(ids_loaded[0], 16)
            w_view = pair_w.rearrange("(q p) d e -> q d p e", q=QUARTERS)
            for k in range(len(LOADS) - 1):
                a, b = LOADS[k] * PIECE, LOADS[k + 1] * PIECE
                for q in range(QUARTERS):
                    sp.dma_start(
                        w_in[q * DIM:(q + 1) * DIM, a * DIM:b * DIM].rearrange("d (p e) -> d p e", e=DIM),
                        w_view[q, :, a:b, :]).then_inc(w_loaded[k], 16)
            sp.dma_start(ids_sb[1][:, :], ids[B:2 * B, :]).then_inc(ids_loaded[1], 16)
            for g in range(K1):
                sp.dma_start(w1_sb[0:k1_rows[g], g, :],
                             w1[sum(k1_rows[:g]):sum(k1_rows[:g + 1]), :]).then_inc(weights_loaded, 16)
            sp.dma_start(w2_sb[:, :, :], w2.rearrange("(k p) n -> p k n", p=128)).then_inc(weights_loaded, 16)
            sp.dma_start(w3_sb[:, :], w3[:, :]).then_inc(weights_loaded, 16)
            sp.dma_start(b1_sb[:, :], b1[:, :]).then_inc(weights_loaded, 16)
            sp.dma_start(b2_sb[:, :], b2[:, :]).then_inc(weights_loaded, 16)

            def tile(it, h):
                row = it * (2 * B) + h * B
                if not isinstance(it, int):
                    row = sp.snap(row)
                if not isinstance(it, int) or it > 0:
                    for u in range(UNITS):
                        sp.wait_ge(x_gathered[h][u], it * (16 * UNIT))
                    sp.sem_inc(sp_steps, 1)
                    sp.dma_start(ids_sb[h][:, :], ids[bass.ds(row, B), :]).then_inc(ids_loaded[h], 16)
                    sp.wait_ge(l1_summed, after(it, h, M1, -M1))
                    sp.sem_inc(sp_steps, 1)
                sp.dma_start(z_t[REST:REST + NDENSE, h, FULL, :],
                             dense_t[:, bass.ds(row, B)]).then_inc(dense_loaded[h], 16)

            tile(0, 0)
            tile(0, 1)
            with sp.Fori(1, PAIRS_OF_TILES) as it:
                tile(it, 0)
                tile(it, 1)

        @block.gpsimd
        def _(pool):
            nc.gpsimd.memset(ident[:, :], 1.0).then_inc(ident_made, 1)
            pool.wait_ge(ident_made, 1)
            nc.gpsimd.affine_select(out=ident[:, :], in_=ident[:, :], compare_op=ALU.is_equal, fill=0.0,
                                    base=0, pattern=[[1, 128]], channel_multiplier=-1).then_inc(ident_made, 1)

            def tile(it, h):
                pool.wait_ge(ids_loaded[h], (it + 1) * 16)
                for u in range(UNITS):
                    wait(pool, multiplied, after(it, h, CHUNKS, mixed[u] + 1 - 2 * CHUNKS))
                    pool.sem_inc(pool_steps, 1)
                    for f in range(u * UNIT, (u + 1) * UNIT):
                        pool.indirect_dma_start(
                            x_rows[h][:, f * DIM:(f + 1) * DIM], None, tables[f],
                            bass.IndirectOffsetOnAxis(ap=ids_sb[h][:, f:f + 1], axis=0)
                        ).then_inc(x_gathered[h][u], 16)

            tile(0, 0)
            tile(0, 1)
            with pool.Fori(1, PAIRS_OF_TILES) as it:
                tile(it, 0)
                tile(it, 1)

        @block.scalar
        def _(act):
            act.wait_ge(ident_made, 2)
            nc.scalar.activation(ident_r[:, :], ident[:, :], ACT.Copy).then_inc(ident_r_made, 1)

            def field_view(h, u):
                return x_rows[h][:, u * UNIT * DIM:(u + 1) * UNIT * DIM].rearrange("p (f d) -> p f d", d=DIM)

            def split_unit(it, h, u):
                s = (UNITS * h + u) % 2
                act.wait_ge(x_gathered[h][u], (it + 1) * (16 * UNIT))
                wait(act, xt_made, after(it, h, UNITS, u - 1))
                nc.scalar.activation(x_split[:, s, :, 0, :], field_view(h, u), ACT.Copy).then_inc(hi_made, 1)

            def stack_unit(it, h, u):
                act.wait_ge(xt_made, after(it, h, UNITS, u + 1))
                for a in range(2):
                    for b in range(2):
                        last = nc.scalar.activation(
                            x_stack[b * 64:(b + 1) * 64, u * UNIT:(u + 1) * UNIT, :]
                            .rearrange("p (k a) b -> p a k b", a=2)[:, a],
                            xt_ps[a * 64:(a + 1) * 64, :, :], ACT.Copy)
                last.then_inc(x_stacked, 1)

            def store_z(it, h, g):
                act.wait_ge(z_summed, after(it, h, GROUPS, g + 1))
                if g == 0:
                    wait(act, l1_summed, after(it, h, M1, -M1))
                nc.scalar.activation(z_t[0:group_size[g], h, g, :], z_ps[g % 2][0:group_size[g], 0, :],
                                     ACT.Copy).then_inc(z_stored, 1)

            def store_h1(it, h, m):
                act.wait_ge(l1_summed, after(it, h, M1, M1))
                nc.scalar.activation(h1_t[:, m, :], top_ps[:, m, :], ACT.Relu,
                                     bias=b1_sb[:, m:m + 1]).then_inc(h1_stored, 1)

            def store_h2(it, h, m):
                act.wait_ge(l2_summed, after(it, h, M2, M2))
                nc.scalar.activation(h2_t[:, m, :], top_ps[:, m, :], ACT.Relu,
                                     bias=b2_sb[:, m:m + 1]).then_inc(h2_stored, 1)

            def store_y(it, h, row):
                act.wait_ge(y_summed, after(it, h, 1, 1))
                wait(act, y_written[h], it * 16)
                nc.scalar.activation(y_row[0:1, h, :], top_ps[0:1, 2, :], ACT.Copy).then_inc(y_stored, 1)
                act.wait_ge(y_stored, after(it, h, 1, 1))
                act.dma_start(out[bass.ds(row, B), :].rearrange("b o -> o b"),
                              y_row[0:1, h, :]).then_inc(y_written[h], 16)

            def tile(it, h, before, ahead):
                for s in range(CHUNKS):
                    if s in SPLIT_SLOT:
                        split_unit(it, h, SPLIT_SLOT[s])
                    if ahead and s == NEXT_SPLIT_SLOT:
                        split_unit(*ahead, 0)
                    if s in TURN_SLOT:
                        stack_unit(it, h, TURN_SLOT[s])
                    if ahead and s == NEXT_TURN_SLOT:
                        stack_unit(*ahead, 0)
                    if before and s == CPG - 2:
                        store_z(*before[:2], FULL - 1)
                        store_z(*before[:2], FULL)
                    if s > CPG and s % CPG == CPG - 1:
                        store_z(it, h, s // CPG - 1)
                    if before:
                        if s == LAYER1_END:
                            act.wait_ge(weights_loaded, 16 * (K1 + 4))
                            for m in range(M1):
                                store_h1(*before[:2], m)
                        if s == LAYER2_END:
                            for m in range(M2):
                                store_h2(*before[:2], m)
                        if s == LAYER3_SLOT:
                            store_y(*before)

            def high_s(k):
                act.wait_ge(s_summed, k + 1)
                if k >= RING:
                    act.wait_ge(s_lo_made, k - RING + 1)
                    act.wait_ge(s_spread[1], k - RING + 1)
                nc.scalar.activation(s_hi[k % RING], s_sum[k % RING], ACT.Copy).then_inc(s_hi_made, 1)

            def place_s(k):
                act.wait_ge(s_spread[0], k + 1)
                nc.scalar.activation(stack_part(0, k), spread_part(0, k), ACT.Copy).then_inc(s_placed, 1)
                if k % 2 == 1:
                    act.wait_ge(s_spread[1], k + 1)
                    nc.scalar.activation(stack_part(1, k), spread_part(1, k), ACT.Copy).then_inc(s_placed_act, 1)

            high_s(0)
            for k in range(NPIECE):
                if k + 1 < NPIECE:
                    high_s(k + 1)
                if k == FIRST_TURN - 3:
                    split_unit(0, 0, 0)
                if k >= 1:
                    place_s(k - 1)
                if k == FIRST_TURN:
                    stack_unit(0, 0, 0)
            place_s(NPIECE - 1)

            last = PAIRS_OF_TILES - 1
            tile(0, 0, None, (0, 1))
            tile(0, 1, (0, 0, 0), (1, 0))
            with act.Fori(1, last) as it:
                tile(it, 0, (it - 1, 1, it * (2 * B) - B), (it, 1))
                tile(it, 1, (it, 0, it * (2 * B)), (it + 1, 0))
            tile(last, 0, (last - 1, 1, last * (2 * B) - B), (last, 1))
            tile(last, 1, (last, 0, last * (2 * B)), None)
            store_z(last, 1, FULL - 1)
            store_z(last, 1, FULL)
            for m in range(M1):
                store_h1(last, 1, m)
            for m in range(M2):
                store_h2(last, 1, m)
            store_y(last, 1, BATCH - B)
            for h in range(2):
                act.wait_ge(y_written[h], 16 * (PAIRS_OF_TILES))

        @block.vector
        def _(dve):
            nc.vector.memset(spread.bitcast(F32), 0.0).then_inc(spread_zeroed, 1)
            dve.wait_ge(ident_made, 2)
            dve.wait_ge(spread_zeroed, 1)
            for part in range(2):
                nc.vector.tensor_copy(
                    spread[:, :, part, part * 2 * DIM:(part + 1) * 2 * DIM].rearrange("p q (r d) -> p q r d", r=2),
                    ident[:, :].rearrange("p (q d) -> p q d", q=QUARTERS).unsqueeze(2)
                    .to_broadcast([128, QUARTERS, 2, DIM])).then_inc(spread_made, 1)

            def turned_w(k):
                load = max(n for n in range(len(LOADS) - 1) if LOADS[n] <= k)
                dve.wait_ge(w_loaded[load], 16 * QUARTERS)
                if k >= RING:
                    dve.wait_ge(s_hi_made, k - RING + 1)
                    dve.wait_ge(s_lo_made, k - RING + 1)
                nc.vector.transpose(s_sum[k % RING], w_in[:, k * PC:(k + 1) * PC]).then_inc(w_turned, 1)

            def summed_s(k):
                dve.wait_ge(w_turned, k + 1)
                nc.vector.tensor_tensor(s_sum[k % RING], s_sum[k % RING], w_in[:, k * PC:(k + 1) * PC],
                                        ALU.add).then_inc(s_summed, 1)

            def low_s(k):
                dve.wait_ge(s_summed, k + 1)
                dve.wait_ge(s_hi_made, k + 1)
                if k >= RING:
                    dve.wait_ge(s_spread[1], k - RING + 1)
                nc.vector.tensor_tensor(s_lo[k % RING], s_sum[k % RING], s_hi[k % RING].bitcast(F32),
                                        ALU.subtract).then_inc(s_lo_made, 1)

            def place_s(k):
                dve.wait_ge(s_spread[1], k + 1)
                nc.vector.tensor_copy(stack_part(1, k), spread_part(1, k)).then_inc(s_placed_dve, 1)

            def low_part(it, h, u):
                s = (UNITS * h + u) % 2
                dve.wait_ge(x_gathered[h][u], (it + 1) * (16 * UNIT))
                dve.wait_ge(hi_made, after(it, h, UNITS, u + 1))
                nc.vector.tensor_tensor(
                    x_split[:, s, :, 1, :],
                    x_rows[h][:, u * UNIT * DIM:(u + 1) * UNIT * DIM].rearrange("p (f d) -> p f d", d=DIM),
                    x_split[:, s, :, 0, :].bitcast(F32), ALU.subtract).then_inc(lo_made, 1)

            for k in range(2):
                turned_w(k)
                summed_s(k)
            for k in range(NPIECE):
                low_s(k)
                if k + 2 < NPIECE:
                    turned_w(k + 2)
                    summed_s(k + 2)
                if k == FIRST_TURN - 2:
                    low_part(0, 0, 0)
                if k % 2 == 1:
                    place_s(k - 1)
            place_s(NPIECE - 1)

            def multiply(it, h, c):
                g = c // CPG
                if c % CPG == 0:
                    wait(dve, z_summed, after(it, h, GROUPS, 0 if g == FULL else g - 1 if g >= 2 else g - 2))
                for u in sorted(units_read(c) - set().union(*(units_read(b) for b in range(c)))):
                    dve.wait_ge(x_gathered[h][u], (it + 1) * (16 * UNIT))
                dve.wait_ge(t_made, after(it, h, CHUNKS, c + 1))
                room = products_rest[:, :] if g == FULL else products[:, g % 2, place(c) * DIM:]
                t = prod_ps[(CHUNKS * h + c) % 2]
                _, i0, j0, width, _ = chunks[c][0]
                xj = x_rows[h][:, j0 * DIM:(j0 + width) * DIM].unsqueeze(1)
                if len(chunks[c]) == 1:
                    last = nc.vector.tensor_tensor(
                        room[:, 0:CH * DIM].rearrange("p (r n) -> p r n", r=ROWS),
                        t[:, :].rearrange("p (r n) -> p r n", r=ROWS),
                        xj.to_broadcast([128, ROWS, width * DIM]), ALU.mult)
                else:
                    nc.vector.tensor_tensor(
                        room[:, 0:ROWS * width * DIM].rearrange("p (k r n) -> p k r n", k=2, r=2),
                        t[:, :].rearrange("p (k n) -> p k n", k=2)[:, :, RECT_AT[0] * DIM:]
                        .rearrange("p k (r n) -> p k r n", r=2),
                        xj.unsqueeze(1).to_broadcast([128, 2, 2, width * DIM]), ALU.mult)
                    for r in range(ROWS - 1):
                        n = (ROWS - 1 - r) * DIM
                        to = sum(ROWS - 1 - x for x in range(r)) * DIM
                        at, step = TRI_AT[0][r] * DIM, (TRI_AT[1][r] - TRI_AT[0][r]) * DIM
                        last = nc.vector.tensor_tensor(
                            room[:, ROWS * ROWS * DIM:size[c] * DIM]
                            .rearrange("p (k n) -> p k n", k=2)[:, :, to:to + n],
                            t[:, at:at + 2 * step].rearrange("p (k n) -> p k n", k=2)[:, :, 0:n],
                            x_rows[h][:, i0 * DIM:(i0 + UNIT) * DIM]
                            .rearrange("p (k n) -> p k n", k=2)[:, :, (r + 1) * DIM:], ALU.mult)
                last.then_inc(multiplied, 1)

            def sum_part(it, h, c):
                g = c // CPG
                dve.wait_ge(multiplied, after(it, h, CHUNKS, min(c + RED, CHUNKS)))
                if g < FULL:
                    pairs = slice(place(c), place(c) + sum(size[c:c + RED]))
                    nc.vector.tensor_reduce(
                        partial[:, g % 2, pairs],
                        products[:, g % 2, :].rearrange("p (n e) -> p n e", e=DIM)[:, pairs, 0:E_DVE],
                        AX.X, ALU.add).then_inc(part_summed, 1)
                else:
                    nc.vector.tensor_reduce(
                        partial_rest[:, :], products_rest[:, :].rearrange("p (n e) -> p n e", e=DIM),
                        AX.X, ALU.add).then_inc(part_summed, 1)

            def tile(it, h, ahead):
                for c in range(CHUNKS):
                    multiply(it, h, c)
                    if c in SPLIT_SLOT:
                        low_part(it, h, SPLIT_SLOT[c])
                    if ahead and c == NEXT_SPLIT_SLOT:
                        low_part(*ahead, 0)
                    if c >= RED and c % RED == 0:
                        sum_part(it, h, c - RED)
                sum_part(it, h, CHUNKS - 1)

            last_pair = PAIRS_OF_TILES - 1
            tile(0, 0, (0, 1))
            tile(0, 1, (1, 0))
            with dve.Fori(1, last_pair) as it:
                tile(it, 0, (it, 1))
                tile(it, 1, (it + 1, 0))
            tile(last_pair, 0, (last_pair, 1))
            tile(last_pair, 1, None)

        @block.tensor
        def _(pe):
            def turn_unit(it, h, u):
                s = (UNITS * h + u) % 2
                pe.wait_ge(lo_made, after(it, h, UNITS, u + 1))
                wait(pe, x_stacked, after(it, h, UNITS, u))
                for k in range(UNIT // 2):
                    last = nc.tensor.matmul(
                        xt_ps[:, k, :], x_split[:, s, 2 * k:2 * k + 2, :, :].rearrange("p f r d -> p (f r d)"),
                        ident_r[:, :], start=True, stop=True)
                last.then_inc(xt_made, 1)

            def row_products(it, h, c):
                wait(pe, multiplied, after(it, h, CHUNKS, c - 1))
                i0, j0 = chunks[c][0][1:3]
                pe.wait_ge(x_stacked, after(it, h, UNITS, 1 + i0 // UNIT))
                t = prod_ps[(CHUNKS * h + c) % 2]

                def matmul(i, j, n, at):
                    first = natural(i, j, FIELDS) * DIM
                    return nc.tensor.matmul(t[:, at * DIM:(at + n) * DIM], x_stack[:, i, :],
                                            s_stack[:, first:first + n * DIM], start=True, stop=True)

                if len(chunks[c]) == 1:
                    for r in range(ROWS):
                        last = matmul(i0 + r, j0, WIDE, r * WIDE)
                else:
                    for r in range(ROWS):
                        i = i0 + r
                        apart = j0 - (i + 1)
                        if r < ROWS - 1 and apart >= ROWS:
                            first, at = natural(i, i + 1, FIELDS) * DIM, TRI_AT[0][r] * DIM
                            there = (RECT_AT[r] - TRI_AT[0][r]) * DIM
                            nc.tensor.matmul(
                                t[:, at:at + 2 * there].rearrange("p (k n) -> p k n", k=2)[:, :, 0:ROWS * DIM],
                                x_stack[:, i, :],
                                s_stack[:, first:first + 2 * apart * DIM]
                                .rearrange("p (k n) -> p k n", k=2)[:, :, 0:ROWS * DIM], start=True, stop=True)
                        else:
                            last = matmul(i, j0, ROWS, RECT_AT[r])
                            if r < ROWS - 1:
                                matmul(i, i + 1, ROWS - 1 - r, TRI_AT[0][r])
                    for r in range(ROWS - 1):
                        i = i0 + ROWS + r
                        last = matmul(i, i + 1, ROWS - 1 - r, TRI_AT[1][r])
                last.then_inc(t_made, 1)

            def sum_group(it, h, g, part):
                if part == 0:
                    pe.wait_ge(multiplied, after(it, h, CHUNKS, CPG * (g + 1)))
                    wait(pe, z_stored, after(it, h, GROUPS, g - 1 if g >= 2 else -g))
                n_pairs = group_size[g]
                p = products[:, g % 2, :].rearrange("p (n e) -> p n e", e=DIM)[:, 0:n_pairs, :]
                for n in range(part_at[part], part_at[part + 1]):
                    if n < SUMS - 1:
                        lhs = p[:, :, E_DVE + n]
                    else:
                        pe.wait_ge(part_summed, after(it, h, PARTS, CPG // RED * (g + 1)))
                        lhs = partial[:, g % 2, 0:n_pairs]
                    last = nc.tensor.matmul(z_ps[g % 2][0:n_pairs, 0, :], lhs, ident[:, :],
                                            start=(n == 0), stop=(n == SUMS - 1))
                if part == SUM_PARTS - 1:
                    last.then_inc(z_summed, 1)

            def sum_rest(it, h):
                pe.wait_ge(part_summed, after(it, h, PARTS, PARTS))
                pe.wait_ge(z_stored, after(it, h, GROUPS, FULL - 1))
                nc.tensor.matmul(z_ps[FULL % 2][0:REST, 0, :], partial_rest[:, :], ident[:, :],
                                 start=True, stop=True).then_inc(z_summed, 1)

            def layer1(it, h, step):
                m, k = top1_steps[step]
                if step == 0:
                    pe.wait_ge(weights_loaded, 16 * (K1 + 4))
                    pe.wait_ge(dense_loaded[h], (it + 1) * 16)
                    pe.wait_ge(z_stored, after(it, h, GROUPS, GROUPS))
                    wait(pe, y_stored, after(it, h, 1, 0))
                rows = k1_rows[k]
                last = nc.tensor.matmul(top_ps[:, m, :], w1_sb[0:rows, k, m * 128:(m + 1) * 128],
                                        z_t[0:rows, h, k, :], start=(k == 0), stop=(k == K1 - 1))
                if k == K1 - 1:
                    last.then_inc(l1_summed, 1)

            def layer2(it, h, step):
                m, k = top2_steps[step]
                if step == 0:
                    pe.wait_ge(h1_stored, after(it, h, M1, M1))
                last = nc.tensor.matmul(top_ps[:, m, :], w2_sb[:, k, m * 128:(m + 1) * 128],
                                        h1_t[:, k, :], start=(k == 0), stop=(k == M1 - 1))
                if k == M1 - 1:
                    last.then_inc(l2_summed, 1)

            def layer3(it, h):
                pe.wait_ge(h2_stored, after(it, h, M2, M2))
                for k in range(M2):
                    last = nc.tensor.matmul(top_ps[0:1, 2, :], w3_sb[:, k:k + 1], h2_t[:, k, :],
                                            start=(k == 0), stop=(k == M2 - 1))
                last.then_inc(y_summed, 1)

            def tile(it, h, before, ahead):
                for s in range(CHUNKS):
                    if s in TURN_SLOT:
                        turn_unit(it, h, TURN_SLOT[s])
                    if ahead and s == NEXT_TURN_SLOT:
                        turn_unit(*ahead, 0)
                    row_products(it, h, s)
                    if before:
                        for n in layer_slots[s]:
                            if n < len(top1_steps):
                                layer1(*before, n)
                            else:
                                layer2(*before, n - len(top1_steps))
                    if sums_in(s):
                        back, g, part = sums_in(s)
                        if not back:
                            sum_group(it, h, g, part)
                        elif before:
                            sum_group(*before, g, part)
                    if before and s == CPG - 2:
                        sum_rest(*before)
                    if before and s == LAYER3_SLOT:
                        layer3(*before)

            pe.wait_ge(ident_r_made, 1)
            pe.wait_ge(spread_made, 2)
            for k in range(NPIECE):
                if k >= 2:
                    pe.wait_ge(s_placed, k - 1)
                    if k % 2 == 1:
                        pe.wait_ge(s_placed_act, k // 2)
                    else:
                        pe.wait_ge(s_placed_dve, k // 2)
                if k % 2 == 1 and k > FIRST_TURN:
                    pe.wait_ge(x_stacked, 1)
                pe.wait_ge(s_hi_made, k + 1)
                pe.wait_ge(s_lo_made, k + 1)
                for q in range(QUARTERS):
                    dst = spread_part(q // 2, k)[:, q % 2, :]
                    nc.tensor.matmul(dst, spread[:, q, 0, :], s_hi[k % RING], start=True, stop=False)
                    last = nc.tensor.matmul(dst, spread[:, q, 1, :], s_lo[k % RING], start=False, stop=True)
                    if q % 2 == 1:
                        last.then_inc(s_spread[q // 2], 1)
                if k == FIRST_TURN:
                    pe.wait_ge(s_placed, k)
                    turn_unit(0, 0, 0)

            pe.wait_ge(s_placed, NPIECE)
            pe.wait_ge(s_placed_act, NPIECE // 2)
            pe.wait_ge(s_placed_dve, NPIECE - NPIECE // 2)
            last_pair = PAIRS_OF_TILES - 1
            tile(0, 0, None, (0, 1))
            tile(0, 1, (0, 0), (1, 0))
            with pe.Fori(1, last_pair) as it:
                tile(it, 0, (it - 1, 1), (it, 1))
                tile(it, 1, (it, 0), (it + 1, 0))
            tile(last_pair, 0, (last_pair - 1, 1), (last_pair, 1))
            tile(last_pair, 1, (last_pair, 0), None)
            last_tile = (last_pair, 1)
            for part in range(SUM_PARTS):
                sum_group(*last_tile, FULL - 1, part)
            sum_rest(*last_tile)
            for n in range(len(top1_steps)):
                layer1(*last_tile, n)
            for n in range(len(top2_steps)):
                layer2(*last_tile, n)
            layer3(*last_tile)


N_TABLES = 40


def layer1_order(fields, pairs, features):
    chunks, _ = pair_chunks(fields, 32, 4)
    order = [natural(i, j + n, fields) for c in chunks for i, j, m, _ in strips(c, 4) for n in range(m)]
    return order + list(range(pairs, features))


def kernel(**inputs):
    import numpy as _np
    import concourse.bacc as _bacc
    from concourse import mybir as _mybir
    from concourse.bass_utils import run_bass_kernel_spmd as _run

    nc = _bacc.Bacc("TRN2", target_bir_lowering=False, num_devices=1)
    arrays = {}

    def dram(name, a):
        a = _np.ascontiguousarray(a)
        arrays[name] = a
        return nc.dram_tensor(name, a.shape, _mybir.dt.from_np(a.dtype), kind="ExternalInput").ap()

    ids = dram("ids_dram", inputs["ids"])
    tables = [dram(f"tbl_{f}_dram", inputs[f"tbl_{f}"]) for f in range(N_TABLES)]
    pair_w = dram("pair_w_dram", inputs["L0_rec_W"])
    dense_t = dram("dense_t_dram", _np.asarray(inputs["dense_ctx"]).T)
    w1 = dram("w1_dram", _np.asarray(inputs["W_top1"])[layer1_order(N_TABLES, len(inputs["L0_rec_W"]), len(inputs["W_top1"]))])
    w2 = dram("w2_dram", inputs["W_top2"])
    b1, b2, w3 = (dram(f"{n}_dram", _np.asarray(inputs[n]).reshape(-1, 128).T)
                  for n in ("b_top1", "b_top2", "W_top3"))
    out = nc.dram_tensor("out_0_dram", (ids.shape[0], 1), _mybir.dt.float32, kind="ExternalOutput").ap()
    dlrm_tower_program(nc, ids, tables, pair_w, dense_t, w1, b1, w2, b2, w3, out)
    r = _run(nc, [arrays], core_ids=[0])
    return r.results[0]["out_0_dram"]
```

```python
import concourse.bass as bass
from concourse import mybir
from contextlib import ExitStack

F32 = mybir.dt.float32
F32R = mybir.dt.float32r
I32 = mybir.dt.int32
ALU = mybir.AluOpType
ACT = mybir.ActivationFunctionType
AX = mybir.AxisListType


def natural(i, j, fields):
    return i * fields - i * (i + 1) // 2 + j - i - 1


def pair_chunks(fields, rows):
    unit = 2 * rows
    chunks, last = [], []
    for u in range(0, fields, unit):
        chunks += [("rect", i0, j0) for j0 in range(u + unit, fields, unit) for i0 in (u, u + rows)]
        last.append(len(chunks))
        chunks.append(("tri", u, u))
    return chunks, last


def chunk_pairs(chunk, rows):
    kind, i0, j0 = chunk
    if kind == "rect":
        return [(i0 + r, j0 + n) for r in range(rows) for n in range(2 * rows)]
    pairs = [(i0 + r, i0 + rows + n) for r in range(rows) for n in range(rows)]
    for k in range(2):
        base = i0 + k * rows
        pairs += [(base + r, base + n) for r in range(rows - 1) for n in range(r + 1, rows)]
    return pairs


def dlrm_tower_program(nc, ids, tables, pair_w, dense_t, w1, b1, w2, b2, w3, out):
    BATCH, FIELDS = ids.shape
    PAIRS, DIM, _ = pair_w.shape
    B = 128
    TILES = BATCH // B
    PAIRS_OF_TILES = TILES // 2
    NDENSE = dense_t.shape[0]
    H1, H2 = w1.shape[1], w2.shape[1]
    M1, M2 = H1 // 128, H2 // 128

    CH = 32
    ROWS = 4
    UNIT = 2 * ROWS
    UNITS = FIELDS // UNIT
    chunks, last_chunk = pair_chunks(FIELDS, ROWS)
    CHUNKS = len(chunks)
    size = [len(chunk_pairs(chunk, ROWS)) for chunk in chunks]
    assert sum(size) == PAIRS and max(size) == CH

    def new_unit(c):
        units = [j // UNIT for _, _, j in chunks[:c + 1]]
        return None if units[c] in units[:c] else units[c]

    CPG = 4
    FULL = CHUNKS // CPG
    GROUPS = FULL + 1
    group_size = [sum(size[g * CPG:(g + 1) * CPG]) for g in range(GROUPS)]
    GRP = max(group_size)
    REST = group_size[FULL]
    e_dve = [17] * 4 + [16] * (FULL - 4)
    sums = [DIM - e + 1 for e in e_dve]
    RED = 2
    PARTS = FULL * CPG // RED

    def place(c):
        return sum(size[c // CPG * CPG:c])

    K1 = GROUPS
    k1_rows = group_size[:FULL] + [REST + NDENSE]
    top1_steps = [(m, k) for m in range(M1) for k in range(K1)]
    top2_steps = [(m, k) for m in range(M2) for k in range(M1)]

    TRI_AT = [0, 7, 18, 25, 13, 16, 23]
    RECT_AT = [TRI_AT[r] + ROWS - 1 - r for r in range(ROWS)]

    SPLIT_SLOT = {1: 1, 5: 2, 9: 3, 13: 4}
    TURN_SLOT = {4: 1, 8: 2, 12: 3, 16: 4}
    NEXT_SPLIT_SLOT = 18
    NEXT_TURN_SLOT = 21
    REST_SLOTS = [0, 1, 3]
    REST_TURN_SLOT = 5
    LAYER3_SLOT = 0
    STORE_Y_SLOT = 2
    part_at = [[0] + [2 + (n - 2) * k // (CPG - 1) for k in range(CPG)] for n in sums]

    def sums_in(s):
        if s < CPG:
            return None if s == CPG - 1 else (1, FULL - 1, s + 1)
        return (0, *divmod(s - CPG, CPG))

    def tensor_load(s):
        matmuls = ROWS if chunks[s][0] == "rect" else UNIT - 1
        turns = UNIT // 2 * (s in TURN_SLOT or s == NEXT_TURN_SLOT)
        summed = (s == REST_TURN_SLOT) + M2 * (s == LAYER3_SLOT)
        if sums_in(s):
            _, g, part = sums_in(s)
            summed += part_at[g][part + 1] - part_at[g][part]
        return matmuls + turns + 2 * summed

    def vector_load(s):
        OVERHEAD = 64
        load = size[s] * DIM + OVERHEAD * (1 if chunks[s][0] == "rect" else ROWS)
        load += (UNIT * DIM + OVERHEAD) * (s in SPLIT_SLOT or s == NEXT_SPLIT_SLOT)
        if s >= RED and s % RED == 0:
            load += RED * CH * e_dve[(s - RED) // CPG] + OVERHEAD
        return load

    def plan_layers():
        MOST = 6
        tensor = [tensor_load(s) for s in range(CHUNKS)]
        vector = [vector_load(s) for s in range(CHUNKS)]
        steps = len(top1_steps) + len(top2_steps)
        total = sum(tensor) + 2 * steps
        slots, done, first2 = [], 0, 0
        for s in range(CHUNKS):
            slots.append([])
            room = total * sum(vector[:s + 1]) / sum(vector) - sum(tensor[:s + 1])
            while s >= CPG and done < steps and 2 * (done + 1) <= room and len(slots[s]) < MOST:
                if s <= REST_TURN_SLOT + 1 and done == K1 - 1 or done == len(top1_steps) and s < first2:
                    break
                slots[s].append(done)
                done += 1
                first2 = s + 2 if done == len(top1_steps) else first2
        slots[CHUNKS - 1] += range(done, steps)
        return slots

    layer_slots = plan_layers()
    LAYER1_END = next(s for s in range(CHUNKS) if len(top1_steps) - 1 in layer_slots[s])
    LAYER2_END = next(s for s in range(CHUNKS) if len(top1_steps) + len(top2_steps) - 1 in layer_slots[s])

    QUARTERS = 128 // DIM
    QP = PAIRS // QUARTERS
    PIECE = 15
    NPIECE = QP // PIECE
    PC = PIECE * DIM
    LOADS = [0, 1, 2, 4, 8, NPIECE]
    RING = 3
    FIRST_TURN = 10

    with ExitStack() as ctx:
        def sb(name, shape, dt=F32):
            return ctx.enter_context(nc.sbuf_tensor(name, shape, dt))

        def ps(name, shape):
            return ctx.enter_context(nc.psum_tensor(name, shape, F32))

        def sem(name):
            return ctx.enter_context(nc.semaphore(name))

        s_stack = sb("s_stack", [128, PAIRS * DIM], F32R)
        products = sb("products", [128, 2, GRP * DIM])
        products_rest = sb("products_rest", [128, REST * DIM])
        x_rows = [sb(f"x_rows{h}", [128, FIELDS * DIM]) for h in range(2)]
        x_split = sb("x_split", [128, 2, UNIT, 2, DIM], F32R)
        x_stack = sb("x_stack", [128, FIELDS, B], F32R)
        ids_sb = [sb(f"ids_sb{h}", [128, FIELDS], I32) for h in range(2)]
        partial = sb("partial", [128, 2, GRP])
        partial_rest = sb("partial_rest", [128, REST])
        z_t = sb("z_t", [128, 2, K1, B])
        h1_t = sb("h1_t", [128, M1, B])
        h2_t = sb("h2_t", [128, M2, B])
        y_row = sb("y_row", [1, 2, B])
        w1_sb = sb("w1_sb", [128, K1, H1])
        w2_sb = sb("w2_sb", [128, M1, H2])
        w3_sb = sb("w3_sb", [128, M2])
        b1_sb = sb("b1_sb", [128, M1])
        b2_sb = sb("b2_sb", [128, M2])
        ident = sb("ident", [128, 128])
        ident_r = sb("ident_r", [128, 128], F32R)

        room = products[:, :, :].rearrange("p a n -> p (a n)")
        w_in = room[:, 0:QP * DIM]
        s_sum = [room[:, QP * DIM + k * PC:QP * DIM + (k + 1) * PC] for k in range(RING)]
        room_r = x_stack[:, UNIT:, :].rearrange("p f b -> p (f b)")
        base = QUARTERS * 2 * 128
        spread = room_r[:, 0:base].rearrange("p (q l m) -> p q l m", q=QUARTERS, l=2)
        s_hi = [room_r[:, base + k * PC:base + (k + 1) * PC] for k in range(RING)]
        s_lo = [room_r[:, base + (RING + k) * PC:base + (RING + k + 1) * PC] for k in range(RING)]

        prod_ps = [ps(f"prod_ps{k}", [128, CH * DIM]) for k in range(2)]
        other_ps = [ps(f"other_ps{k}", [128, 2, 4, B]) for k in range(2)]
        xt_ps, top_ps = other_ps[0][:, 0], other_ps[0][:, 1]
        z_ps = [other_ps[1][:, min(g, FULL - 1) % 2] for g in range(GROUPS)]

        ids_loaded = [sem(f"ids_loaded{h}") for h in range(2)]
        x_gathered = [[sem(f"x_gathered{h}_{u}") for u in range(UNITS)] for h in range(2)]
        dense_loaded = [sem(f"dense_loaded{h}") for h in range(2)]
        w_loaded = [sem(f"w_loaded{k}") for k in range(len(LOADS) - 1)]
        w_turned = sem("w_turned")
        s_summed = sem("s_summed")
        s_hi_made = sem("s_hi_made")
        s_lo_made = sem("s_lo_made")
        spread_zeroed = sem("spread_zeroed")
        spread_made = sem("spread_made")
        s_spread = [sem(f"s_spread{k}") for k in range(2)]
        s_placed = sem("s_placed")
        s_placed_act = sem("s_placed_act")
        s_placed_dve = sem("s_placed_dve")
        pool_steps = sem("pool_steps")
        sp_steps = sem("sp_steps")
        weights_loaded = sem("weights_loaded")
        ident_made = sem("ident_made")
        ident_r_made = sem("ident_r_made")
        hi_made = sem("hi_made")
        lo_made = sem("lo_made")
        xt_made = sem("xt_made")
        x_stacked = sem("x_stacked")
        t_made = sem("t_made")
        multiplied = sem("multiplied")
        part_summed = sem("part_summed")
        rest_summed = sem("rest_summed")
        z_summed = sem("z_summed")
        z_stored = sem("z_stored")
        l1_summed = sem("l1_summed")
        h1_stored = sem("h1_stored")
        l2_summed = sem("l2_summed")
        h2_stored = sem("h2_stored")
        y_summed = sem("y_summed")
        y_stored = sem("y_stored")
        y_written = [sem(f"y_written{h}") for h in range(2)]

        def after(it, h, per_tile, n):
            return it * (2 * per_tile) + (h * per_tile + n)

        def wait(engine, semaphore, value):
            if not isinstance(value, int) or value > 0:
                engine.wait_ge(semaphore, value)

        def stack_part(half, k):
            at = s_stack[:, :].rearrange("r (p q e) -> r q p e", q=QUARTERS, e=DIM)
            return at[:, 2 * half:2 * half + 2, k * PIECE:(k + 1) * PIECE, :]

        def spread_part(half, k):
            if k % 2 == 0:
                both = prod_ps[half][:, :].rearrange("r (q n) -> r q n", q=2)
            else:
                both = other_ps[half][:, :, :, :].rearrange("r q a b -> r q (a b)")
            return both[:, :, 0:PC]

        def by_pair(part):
            return part.rearrange("r q (p e) -> r q p e", e=DIM)

        end_ps = [prod_ps[(CHUNKS + CHUNKS - 2 + k) % 2][:, n * 16 * DIM:n * 16 * DIM + B]
                  for k in range(2) for n in range(2)]
        layer1_ps = [top_ps[:, 0, :], xt_ps[:, 0, :]] + end_ps[0:2]
        layer2_ps = end_ps[2:4]

        block = ctx.enter_context(nc.Block())

        @block.sync
        def _(sp):
            sp.dma_start(ids_sb[0][:, :], ids[0:B, :]).then_inc(ids_loaded[0], 16)
            w_view = pair_w.rearrange("(p q) d e -> (q d) p e", q=QUARTERS)
            for k in range(len(LOADS) - 1):
                a, b = LOADS[k] * PIECE, LOADS[k + 1] * PIECE
                sp.dma_start(w_in[:, a * DIM:b * DIM].rearrange("r (p e) -> r p e", e=DIM),
                             w_view[:, a:b, :]).then_inc(w_loaded[k], 16)
            sp.dma_start(ids_sb[1][:, :], ids[B:2 * B, :]).then_inc(ids_loaded[1], 16)
            for g in range(K1):
                sp.dma_start(w1_sb[0:k1_rows[g], g, :],
                             w1[sum(k1_rows[:g]):sum(k1_rows[:g + 1]), :]).then_inc(weights_loaded, 16)
            sp.dma_start(w2_sb[:, :, :], w2.rearrange("(k p) n -> p k n", p=128)).then_inc(weights_loaded, 16)
            sp.dma_start(w3_sb[:, :], w3[:, :]).then_inc(weights_loaded, 16)
            sp.dma_start(b1_sb[:, :], b1[:, :]).then_inc(weights_loaded, 16)
            sp.dma_start(b2_sb[:, :], b2[:, :]).then_inc(weights_loaded, 16)

            def tile(it, h):
                row = it * (2 * B) + h * B
                if not isinstance(it, int):
                    row = sp.snap(row)
                if not isinstance(it, int) or it > 0:
                    for u in range(UNITS):
                        sp.wait_ge(x_gathered[h][u], it * (16 * UNIT))
                    sp.sem_inc(sp_steps, 1)
                    sp.dma_start(ids_sb[h][:, :], ids[bass.ds(row, B), :]).then_inc(ids_loaded[h], 16)
                    sp.wait_ge(l1_summed, after(it, h, M1, -M1))
                    sp.sem_inc(sp_steps, 1)
                sp.dma_start(z_t[REST:REST + NDENSE, h, FULL, :],
                             dense_t[:, bass.ds(row, B)]).then_inc(dense_loaded[h], 16)

            tile(0, 0)
            tile(0, 1)
            with sp.Fori(1, PAIRS_OF_TILES) as it:
                tile(it, 0)
                tile(it, 1)

        @block.gpsimd
        def _(pool):
            nc.gpsimd.memset(ident[:, :], 1.0).then_inc(ident_made, 1)
            pool.wait_ge(ident_made, 1)
            nc.gpsimd.affine_select(out=ident[:, :], in_=ident[:, :], compare_op=ALU.is_equal, fill=0.0,
                                    base=0, pattern=[[1, 128]], channel_multiplier=-1).then_inc(ident_made, 1)

            def tile(it, h):
                pool.wait_ge(ids_loaded[h], (it + 1) * 16)
                for u in range(UNITS):
                    wait(pool, multiplied, after(it, h, CHUNKS, last_chunk[u] + 1 - 2 * CHUNKS))
                    pool.sem_inc(pool_steps, 1)
                    for f in range(u * UNIT, (u + 1) * UNIT):
                        pool.indirect_dma_start(
                            x_rows[h][:, f * DIM:(f + 1) * DIM], None, tables[f],
                            bass.IndirectOffsetOnAxis(ap=ids_sb[h][:, f:f + 1], axis=0)
                        ).then_inc(x_gathered[h][u], 16)

            tile(0, 0)
            tile(0, 1)
            with pool.Fori(1, PAIRS_OF_TILES) as it:
                tile(it, 0)
                tile(it, 1)

        @block.scalar
        def _(act):
            act.wait_ge(ident_made, 2)
            nc.scalar.activation(ident_r[:, :], ident[:, :], ACT.Copy).then_inc(ident_r_made, 1)

            def field_view(h, u):
                return x_rows[h][:, u * UNIT * DIM:(u + 1) * UNIT * DIM].rearrange("p (f d) -> p f d", d=DIM)

            def split_unit(it, h, u):
                s = (UNITS * h + u) % 2
                act.wait_ge(x_gathered[h][u], (it + 1) * (16 * UNIT))
                wait(act, xt_made, after(it, h, UNITS, u - 1))
                nc.scalar.activation(x_split[:, s, :, 0, :], field_view(h, u), ACT.Copy).then_inc(hi_made, 1)

            def stack_unit(it, h, u):
                act.wait_ge(xt_made, after(it, h, UNITS, u + 1))
                for a in range(2):
                    for b in range(2):
                        last = nc.scalar.activation(
                            x_stack[b * 64:(b + 1) * 64, u * UNIT:(u + 1) * UNIT, :]
                            .rearrange("p (k a) b -> p a k b", a=2)[:, a],
                            xt_ps[a * 64:(a + 1) * 64, :, :], ACT.Copy)
                last.then_inc(x_stacked, 1)

            def sum_last_chunk(it, h, part):
                if part == 0:
                    act.wait_ge(multiplied, after(it, h, CHUNKS, CHUNKS))
                    wait(act, z_summed, after(it, h, GROUPS, 0))
                parts = len(REST_SLOTS)
                for n in range(part * REST // parts, (part + 1) * REST // parts):
                    pair = products_rest[:, n * DIM:(n + 1) * DIM]
                    last = nc.scalar.activation(pair, pair, ACT.Copy, accum_out=partial_rest[:, n:n + 1])
                if part == parts - 1:
                    last.then_inc(rest_summed, 1)

            def store_z(it, h, g):
                act.wait_ge(z_summed, after(it, h, GROUPS, g + 1))
                if g == 0:
                    wait(act, l1_summed, after(it, h, M1, -M1))
                nc.scalar.activation(z_t[0:group_size[g], h, g, :], z_ps[g][0:group_size[g], 0, :],
                                     ACT.Copy).then_inc(z_stored, 1)

            def store_h1(it, h, m, summed=M1, bank=None):
                act.wait_ge(l1_summed, after(it, h, M1, summed))
                nc.scalar.activation(h1_t[:, m, :], top_ps[:, m, :] if bank is None else bank, ACT.Relu,
                                     bias=b1_sb[:, m:m + 1]).then_inc(h1_stored, 1)

            def store_h2(it, h, m, summed=M2, bank=None):
                act.wait_ge(l2_summed, after(it, h, M2, summed))
                nc.scalar.activation(h2_t[:, m, :], top_ps[:, m, :] if bank is None else bank, ACT.Relu,
                                     bias=b2_sb[:, m:m + 1]).then_inc(h2_stored, 1)

            def store_y(it, h):
                act.wait_ge(y_summed, after(it, h, 1, 1))
                wait(act, y_written[h], it * 16)
                nc.scalar.activation(y_row[0:1, h, :], top_ps[0:1, 2, :], ACT.Copy).then_inc(y_stored, 1)
                row = it * (2 * B) + h * B
                if not isinstance(it, int):
                    row = act.snap(row)
                act.wait_ge(y_stored, after(it, h, 1, 1))
                act.dma_start(out[bass.ds(row, B), :].rearrange("b o -> o b"),
                              y_row[0:1, h, :]).then_inc(y_written[h], 16)

            def tile(it, h, older, before, ahead):
                for s in range(CHUNKS):
                    if s in SPLIT_SLOT:
                        split_unit(it, h, SPLIT_SLOT[s])
                    if ahead and s == NEXT_SPLIT_SLOT:
                        split_unit(*ahead, 0)
                    if s in TURN_SLOT:
                        stack_unit(it, h, TURN_SLOT[s])
                    if ahead and s == NEXT_TURN_SLOT:
                        stack_unit(*ahead, 0)
                    if before and s == CPG - 2:
                        store_z(*before, FULL - 1)
                    if before and s == REST_TURN_SLOT:
                        store_z(*before, FULL)
                    if s > CPG and s % CPG == CPG - 1:
                        store_z(it, h, s // CPG - 1)
                    if older and s == STORE_Y_SLOT:
                        store_y(*older)
                    if before and s == LAYER1_END:
                        act.wait_ge(weights_loaded, 16 * (K1 + 4))
                        for m in range(M1):
                            store_h1(*before, m)
                    if before and s == LAYER2_END:
                        for m in range(M2):
                            store_h2(*before, m)
                    if before and s in REST_SLOTS:
                        sum_last_chunk(*before, REST_SLOTS.index(s))

            def high_s(k):
                act.wait_ge(s_summed, k + 1)
                if k >= RING:
                    act.wait_ge(s_lo_made, k - RING + 1)
                    act.wait_ge(s_spread[1], k - RING + 1)
                nc.scalar.activation(s_hi[k % RING], s_sum[k % RING], ACT.Copy).then_inc(s_hi_made, 1)

            def place_s(k):
                act.wait_ge(s_spread[0], k + 1)
                nc.scalar.activation(stack_part(0, k), by_pair(spread_part(0, k)), ACT.Copy).then_inc(s_placed, 1)
                if k % 2 == 1:
                    act.wait_ge(s_spread[1], k + 1)
                    nc.scalar.activation(stack_part(1, k), by_pair(spread_part(1, k)), ACT.Copy).then_inc(s_placed_act, 1)

            high_s(0)
            for k in range(NPIECE):
                if k + 1 < NPIECE:
                    high_s(k + 1)
                if k == FIRST_TURN - 2:
                    split_unit(0, 0, 0)
                if k == FIRST_TURN + 1:
                    stack_unit(0, 0, 0)
                if k >= 1:
                    place_s(k - 1)
            place_s(NPIECE - 1)

            last = PAIRS_OF_TILES - 1
            tile(0, 0, None, None, (0, 1))
            tile(0, 1, None, (0, 0), (1, 0))
            with act.Fori(1, last) as it:
                tile(it, 0, (it - 1, 0), (it - 1, 1), (it, 1))
                tile(it, 1, (it - 1, 1), (it, 0), (it + 1, 0))
            tile(last, 0, (last - 1, 0), (last - 1, 1), (last, 1))
            tile(last, 1, (last - 1, 1), (last, 0), None)
            store_y(last, 0)
            store_z(last, 1, FULL - 1)
            store_z(last, 1, FULL)
            for m in range(M1):
                store_h1(last, 1, m, m + 1, layer1_ps[m])
            for m in range(M2):
                store_h2(last, 1, m, m + 1, layer2_ps[m])
            store_y(last, 1)
            for h in range(2):
                act.wait_ge(y_written[h], 16 * (PAIRS_OF_TILES))

        @block.vector
        def _(dve):
            nc.vector.memset(spread.bitcast(F32), 0.0).then_inc(spread_zeroed, 1)
            dve.wait_ge(ident_made, 2)
            dve.wait_ge(spread_zeroed, 1)
            for part in range(2):
                nc.vector.tensor_copy(
                    spread[:, :, part, part * 2 * DIM:(part + 1) * 2 * DIM].rearrange("p q (r d) -> p q r d", r=2),
                    ident[:, :].rearrange("p (q d) -> p q d", q=QUARTERS).unsqueeze(2)
                    .to_broadcast([128, QUARTERS, 2, DIM])).then_inc(spread_made, 1)

            def turned_w(k):
                load = max(n for n in range(len(LOADS) - 1) if LOADS[n] <= k)
                dve.wait_ge(w_loaded[load], 16)
                if k >= RING:
                    dve.wait_ge(s_hi_made, k - RING + 1)
                    dve.wait_ge(s_lo_made, k - RING + 1)
                nc.vector.transpose(s_sum[k % RING], w_in[:, k * PC:(k + 1) * PC]).then_inc(w_turned, 1)

            def summed_s(k):
                dve.wait_ge(w_turned, k + 1)
                nc.vector.tensor_tensor(s_sum[k % RING], s_sum[k % RING], w_in[:, k * PC:(k + 1) * PC],
                                        ALU.add).then_inc(s_summed, 1)

            def low_s(k):
                dve.wait_ge(s_summed, k + 1)
                dve.wait_ge(s_hi_made, k + 1)
                if k >= RING:
                    dve.wait_ge(s_spread[1], k - RING + 1)
                nc.vector.tensor_tensor(s_lo[k % RING], s_sum[k % RING], s_hi[k % RING].bitcast(F32),
                                        ALU.subtract).then_inc(s_lo_made, 1)

            def place_s(k):
                dve.wait_ge(s_spread[1], k + 1)
                nc.vector.tensor_copy(stack_part(1, k), by_pair(spread_part(1, k))).then_inc(s_placed_dve, 1)

            def low_part(it, h, u):
                s = (UNITS * h + u) % 2
                dve.wait_ge(x_gathered[h][u], (it + 1) * (16 * UNIT))
                dve.wait_ge(hi_made, after(it, h, UNITS, u + 1))
                nc.vector.tensor_tensor(
                    x_split[:, s, :, 1, :],
                    x_rows[h][:, u * UNIT * DIM:(u + 1) * UNIT * DIM].rearrange("p (f d) -> p f d", d=DIM),
                    x_split[:, s, :, 0, :].bitcast(F32), ALU.subtract).then_inc(lo_made, 1)

            for k in range(2):
                turned_w(k)
                summed_s(k)
            for k in range(NPIECE):
                low_s(k)
                if k + 2 < NPIECE:
                    turned_w(k + 2)
                    summed_s(k + 2)
                if k == FIRST_TURN - 1:
                    low_part(0, 0, 0)
                if k % 2 == 1:
                    place_s(k - 1)
            place_s(NPIECE - 1)

            def multiply(it, h, c):
                g = c // CPG
                if c % CPG == 0:
                    wait(dve, z_summed, after(it, h, GROUPS, 0 if g == FULL else g - 1 if g >= 2 else g - 2))
                if new_unit(c) is not None:
                    dve.wait_ge(x_gathered[h][new_unit(c)], (it + 1) * (16 * UNIT))
                dve.wait_ge(t_made, after(it, h, CHUNKS, c + 1))
                room = products_rest[:, :] if g == FULL else products[:, g % 2, place(c) * DIM:]
                t = prod_ps[(CHUNKS * h + c) % 2]
                kind, i0, j0 = chunks[c]
                if kind == "rect":
                    last = nc.vector.tensor_tensor(
                        room[:, 0:CH * DIM].rearrange("p (r n) -> p r n", r=ROWS),
                        t[:, :].rearrange("p (r n) -> p r n", r=ROWS),
                        x_rows[h][:, j0 * DIM:(j0 + UNIT) * DIM].unsqueeze(1)
                        .to_broadcast([128, ROWS, UNIT * DIM]), ALU.mult)
                else:
                    step = (RECT_AT[1] - RECT_AT[0]) * DIM
                    nc.vector.tensor_tensor(
                        room[:, 0:ROWS * ROWS * DIM].rearrange("p (k r n) -> p k r n", k=2, r=2),
                        t[:, :].rearrange("p (k n) -> p k n", k=2)[
                            :, :, RECT_AT[0] * DIM:RECT_AT[0] * DIM + 2 * step]
                        .rearrange("p k (r n) -> p k r n", r=2)[:, :, :, 0:ROWS * DIM],
                        x_rows[h][:, (i0 + ROWS) * DIM:(i0 + UNIT) * DIM].unsqueeze(1).unsqueeze(1)
                        .to_broadcast([128, 2, 2, ROWS * DIM]), ALU.mult)
                    for r in range(ROWS - 1):
                        n = (ROWS - 1 - r) * DIM
                        to = sum(ROWS - 1 - x for x in range(r)) * DIM
                        at, step = TRI_AT[r] * DIM, (TRI_AT[ROWS + r] - TRI_AT[r]) * DIM
                        last = nc.vector.tensor_tensor(
                            room[:, ROWS * ROWS * DIM:size[c] * DIM]
                            .rearrange("p (k n) -> p k n", k=2)[:, :, to:to + n],
                            t[:, at:at + 2 * step].rearrange("p (k n) -> p k n", k=2)[:, :, 0:n],
                            x_rows[h][:, i0 * DIM:(i0 + UNIT) * DIM]
                            .rearrange("p (k n) -> p k n", k=2)[:, :, (r + 1) * DIM:], ALU.mult)
                last.then_inc(multiplied, 1)

            def sum_part(it, h, c):
                g = c // CPG
                dve.wait_ge(multiplied, after(it, h, CHUNKS, c + RED))
                pairs = slice(place(c), place(c) + sum(size[c:c + RED]))
                nc.vector.tensor_reduce(
                    partial[:, g % 2, pairs],
                    products[:, g % 2, :].rearrange("p (n e) -> p n e", e=DIM)[:, pairs, 0:e_dve[g]],
                    AX.X, ALU.add).then_inc(part_summed, 1)

            def tile(it, h, ahead):
                for c in range(CHUNKS):
                    multiply(it, h, c)
                    if c in SPLIT_SLOT:
                        low_part(it, h, SPLIT_SLOT[c])
                    if ahead and c == NEXT_SPLIT_SLOT:
                        low_part(*ahead, 0)
                    if c >= RED and c % RED == 0:
                        sum_part(it, h, c - RED)

            last_pair = PAIRS_OF_TILES - 1
            tile(0, 0, (0, 1))
            tile(0, 1, (1, 0))
            with dve.Fori(1, last_pair) as it:
                tile(it, 0, (it, 1))
                tile(it, 1, (it + 1, 0))
            tile(last_pair, 0, (last_pair, 1))
            tile(last_pair, 1, None)
            dve.wait_ge(multiplied, after(last_pair, 1, CHUNKS, CHUNKS))
            dve.wait_ge(z_summed, after(last_pair, 1, GROUPS, 0))
            nc.vector.tensor_reduce(
                partial_rest[:, :], products_rest[:, :].rearrange("p (n e) -> p n e", e=DIM),
                AX.X, ALU.add).then_inc(rest_summed, 1)

        @block.tensor
        def _(pe):
            def turn_unit(it, h, u):
                s = (UNITS * h + u) % 2
                pe.wait_ge(lo_made, after(it, h, UNITS, u + 1))
                wait(pe, x_stacked, after(it, h, UNITS, u))
                for k in range(UNIT // 2):
                    last = nc.tensor.matmul(
                        xt_ps[:, k, :], x_split[:, s, 2 * k:2 * k + 2, :, :].rearrange("p f r d -> p (f r d)"),
                        ident_r[:, :], start=True, stop=True)
                last.then_inc(xt_made, 1)

            def row_products(it, h, c):
                wait(pe, multiplied, after(it, h, CHUNKS, c - 1))
                kind, i0, j0 = chunks[c]
                pe.wait_ge(x_stacked, after(it, h, UNITS, 1 + i0 // UNIT))
                if h == 0 and c == 1 and isinstance(it, int) and it == 0:
                    pe.wait_ge(s_placed_act, NPIECE // 2)
                    pe.wait_ge(s_placed_dve, NPIECE - NPIECE // 2)
                t = prod_ps[(CHUNKS * h + c) % 2]

                def matmul(i, j, n, at):
                    first = natural(i, j, FIELDS) * DIM
                    return nc.tensor.matmul(t[:, at * DIM:(at + n) * DIM], x_stack[:, i, :],
                                            s_stack[:, first:first + n * DIM], start=True, stop=True)

                if kind == "rect":
                    for r in range(ROWS):
                        last = matmul(i0 + r, j0, UNIT, r * UNIT)
                else:
                    for r in range(UNIT - 1):
                        last = matmul(i0 + r, i0 + r + 1, UNIT - 1 - r, TRI_AT[r])
                last.then_inc(t_made, 1)

            def sum_group(it, h, g, part):
                if part == 0:
                    pe.wait_ge(multiplied, after(it, h, CHUNKS, CPG * (g + 1)))
                    wait(pe, z_stored, after(it, h, GROUPS, g - 1 if g >= 2 else 0 if g == 1 else -2))
                n_pairs = group_size[g]
                p = products[:, g % 2, :].rearrange("p (n e) -> p n e", e=DIM)[:, 0:n_pairs, :]
                for n in range(part_at[g][part], part_at[g][part + 1]):
                    if n < sums[g] - 1:
                        lhs = p[:, :, e_dve[g] + n]
                    else:
                        pe.wait_ge(part_summed, after(it, h, PARTS, CPG // RED * (g + 1)))
                        lhs = partial[:, g % 2, 0:n_pairs]
                    last = nc.tensor.matmul(z_ps[g][0:n_pairs, 0, :], lhs, ident[:, :],
                                            start=(n == 0), stop=(n == sums[g] - 1))
                if part == CPG - 1:
                    last.then_inc(z_summed, 1)

            def sum_rest(it, h):
                pe.wait_ge(rest_summed, after(it, h, 1, 1))
                pe.wait_ge(z_stored, after(it, h, GROUPS, FULL))
                nc.tensor.matmul(z_ps[FULL][0:REST, 0, :], partial_rest[:, :], ident[:, :],
                                 start=True, stop=True).then_inc(z_summed, 1)

            def layer1(it, h, step):
                m, k = top1_steps[step]
                if step == 0:
                    pe.wait_ge(weights_loaded, 16 * (K1 + 4))
                    pe.wait_ge(dense_loaded[h], (it + 1) * 16)
                    pe.wait_ge(z_stored, after(it, h, GROUPS, FULL))
                    wait(pe, y_stored, after(it, h, 1, 0))
                if step == K1 - 1:
                    pe.wait_ge(z_stored, after(it, h, GROUPS, GROUPS))
                rows = k1_rows[k]
                last = nc.tensor.matmul(top_ps[:, m, :], w1_sb[0:rows, k, m * 128:(m + 1) * 128],
                                        z_t[0:rows, h, k, :], start=(k == 0), stop=(k == K1 - 1))
                if k == K1 - 1:
                    last.then_inc(l1_summed, 1)

            def layer2(it, h, step):
                m, k = top2_steps[step]
                if step == 0:
                    pe.wait_ge(h1_stored, after(it, h, M1, M1))
                last = nc.tensor.matmul(top_ps[:, m, :], w2_sb[:, k, m * 128:(m + 1) * 128],
                                        h1_t[:, k, :], start=(k == 0), stop=(k == M1 - 1))
                if k == M1 - 1:
                    last.then_inc(l2_summed, 1)

            def layer3(it, h):
                pe.wait_ge(h2_stored, after(it, h, M2, M2))
                for k in range(M2):
                    last = nc.tensor.matmul(top_ps[0:1, 2, :], w3_sb[:, k:k + 1], h2_t[:, k, :],
                                            start=(k == 0), stop=(k == M2 - 1))
                last.then_inc(y_summed, 1)

            def tile(it, h, older, before, ahead):
                for s in range(CHUNKS):
                    if s in TURN_SLOT:
                        turn_unit(it, h, TURN_SLOT[s])
                    if ahead and s == NEXT_TURN_SLOT:
                        turn_unit(*ahead, 0)
                    row_products(it, h, s)
                    if older and s == LAYER3_SLOT:
                        layer3(*older)
                    if before and s == REST_TURN_SLOT:
                        sum_rest(*before)
                    if before:
                        for n in layer_slots[s]:
                            if n < len(top1_steps):
                                layer1(*before, n)
                            else:
                                layer2(*before, n - len(top1_steps))
                    if sums_in(s):
                        back, g, part = sums_in(s)
                        if not back:
                            sum_group(it, h, g, part)
                        elif before:
                            sum_group(*before, g, part)

            pe.wait_ge(ident_r_made, 1)
            pe.wait_ge(spread_made, 2)
            for k in range(NPIECE):
                if k >= 2:
                    pe.wait_ge(s_placed, k - 1)
                    if k % 2 == 1:
                        pe.wait_ge(s_placed_act, k // 2)
                    else:
                        pe.wait_ge(s_placed_dve, k // 2)
                if k % 2 == 1 and k > FIRST_TURN:
                    pe.wait_ge(x_stacked, 1)
                pe.wait_ge(s_hi_made, k + 1)
                pe.wait_ge(s_lo_made, k + 1)
                for q in range(QUARTERS):
                    dst = spread_part(q // 2, k)[:, q % 2, :]
                    nc.tensor.matmul(dst, spread[:, q, 0, :], s_hi[k % RING], start=True, stop=False)
                    last = nc.tensor.matmul(dst, spread[:, q, 1, :], s_lo[k % RING], start=False, stop=True)
                    if q % 2 == 1:
                        last.then_inc(s_spread[q // 2], 1)
                if k == FIRST_TURN:
                    pe.wait_ge(s_placed, k)
                    turn_unit(0, 0, 0)

            pe.wait_ge(s_placed, NPIECE)
            last_pair = PAIRS_OF_TILES - 1
            tile(0, 0, None, None, (0, 1))
            tile(0, 1, None, (0, 0), (1, 0))
            with pe.Fori(1, last_pair) as it:
                tile(it, 0, (it - 1, 0), (it - 1, 1), (it, 1))
                tile(it, 1, (it - 1, 1), (it, 0), (it + 1, 0))
            tile(last_pair, 0, (last_pair - 1, 0), (last_pair - 1, 1), (last_pair, 1))
            tile(last_pair, 1, (last_pair - 1, 1), (last_pair, 0), None)
            layer3(last_pair, 0)
            last_tile = (last_pair, 1)
            for part in range(1, CPG):
                sum_group(*last_tile, FULL - 1, part)

            def end_layer1(m, k):
                last = nc.tensor.matmul(layer1_ps[m], w1_sb[0:k1_rows[k], k, m * 128:(m + 1) * 128],
                                        z_t[0:k1_rows[k], 1, k, :], start=(k == 0), stop=(k == K1 - 1))
                if k == K1 - 1:
                    last.then_inc(l1_summed, 1)

            pe.wait_ge(z_stored, after(*last_tile, GROUPS, FULL - 1))
            pe.wait_ge(dense_loaded[1], PAIRS_OF_TILES * 16)
            pe.wait_ge(y_stored, after(*last_tile, 1, 0))
            pe.wait_ge(x_stacked, after(*last_tile, UNITS, UNITS))
            pe.wait_ge(multiplied, after(*last_tile, CHUNKS, CHUNKS))
            for k in range(FULL - 1):
                for m in range(M1):
                    end_layer1(m, k)
            sum_rest(*last_tile)
            for m in range(M1):
                end_layer1(m, FULL - 1)
            pe.wait_ge(z_stored, after(*last_tile, GROUPS, GROUPS))
            for m in range(M1):
                end_layer1(m, FULL)
            for k in range(M1):
                pe.wait_ge(h1_stored, after(*last_tile, M1, k + 1))
                for m in range(M2):
                    last = nc.tensor.matmul(layer2_ps[m], w2_sb[:, k, m * 128:(m + 1) * 128],
                                            h1_t[:, k, :], start=(k == 0), stop=(k == M1 - 1))
                    if k == M1 - 1:
                        last.then_inc(l2_summed, 1)
            layer3(*last_tile)


N_TABLES = 40


def layer1_order(fields, pairs, features):
    ROWS = 4
    order = [natural(i, j, fields) for c in pair_chunks(fields, ROWS)[0] for i, j in chunk_pairs(c, ROWS)]
    return order + list(range(pairs, features))


def kernel(**inputs):
    import numpy as _np
    import concourse.bacc as _bacc
    from concourse import mybir as _mybir
    from concourse.bass_utils import run_bass_kernel_spmd as _run

    nc = _bacc.Bacc("TRN2", target_bir_lowering=False, num_devices=1)
    arrays = {}

    def dram(name, a):
        a = _np.ascontiguousarray(a)
        arrays[name] = a
        return nc.dram_tensor(name, a.shape, _mybir.dt.from_np(a.dtype), kind="ExternalInput").ap()

    ids = dram("ids_dram", inputs["ids"])
    tables = [dram(f"tbl_{f}_dram", inputs[f"tbl_{f}"]) for f in range(N_TABLES)]
    pair_w = dram("pair_w_dram", inputs["L0_rec_W"])
    dense_t = dram("dense_t_dram", _np.asarray(inputs["dense_ctx"]).T)
    w1 = dram("w1_dram", _np.asarray(inputs["W_top1"])[layer1_order(N_TABLES, len(inputs["L0_rec_W"]), len(inputs["W_top1"]))])
    w2 = dram("w2_dram", inputs["W_top2"])
    b1, b2, w3 = (dram(f"{n}_dram", _np.asarray(inputs[n]).reshape(-1, 128).T)
                  for n in ("b_top1", "b_top2", "W_top3"))
    out = nc.dram_tensor("out_0_dram", (ids.shape[0], 1), _mybir.dt.float32, kind="ExternalOutput").ap()
    dlrm_tower_program(nc, ids, tables, pair_w, dense_t, w1, b1, w2, b2, w3, out)
    r = _run(nc, [arrays], core_ids=[0])
    return r.results[0]["out_0_dram"]
```
